# Optimizing a Trainium2 kernel written in Bass

```python
import numpy as np
import jax
import jax.numpy as jnp

def _softmax(x, axis=-1):
    return jax.nn.softmax(x, axis=axis)

def _gelu(x):
    return jax.nn.gelu(x, approximate=True)

def _silu(x):
    return jax.nn.silu(x)

def _sigmoid(x):
    return jax.nn.sigmoid(x)

def _layernorm(x, axis=-1, eps=1e-05):
    m = jnp.mean(x, axis=axis, keepdims=True)
    v = jnp.var(x, axis=axis, keepdims=True)
    return (x - m) / jnp.sqrt(v + eps)

def _scatter_add(tgt, idx, src, axis=0):
    return tgt.at[idx].add(src)

def _segment_sum(src, seg, n):
    return jax.ops.segment_sum(src, seg, n)
kernel_name = 'mk_rec_standalone_d1_rec_r8_3dcadc'

def setup_inputs(seed: int=0):
    np.random.seed(seed)
    _w = jnp.asarray

    def _rec_inputs():
        import jax
        import jax.numpy as jnp
        _rk = jax.random.key(seed)
        r_x_num = -0.00338568 + 1.0005 * jax.random.normal(jax.random.fold_in(_rk, 1), (1024, 13), jnp.float32)
        r_x_cat = jnp.stack([jax.random.randint(jax.random.fold_in(jax.random.fold_in(_rk, 2), 0), (1024,), 2, 12500, jnp.int32), jax.random.randint(jax.random.fold_in(jax.random.fold_in(_rk, 2), 1), (1024,), 1, 99999, jnp.int32), jax.random.randint(jax.random.fold_in(jax.random.fold_in(_rk, 2), 2), (1024,), 0, 12500, jnp.int32), jax.random.randint(jax.random.fold_in(jax.random.fold_in(_rk, 2), 3), (1024,), 5, 12500, jnp.int32), jax.random.randint(jax.random.fold_in(jax.random.fold_in(_rk, 2), 4), (1024,), 20, 99993, jnp.int32), jax.random.randint(jax.random.fold_in(jax.random.fold_in(_rk, 2), 5), (1024,), 0, 99993, jnp.int32), jax.random.randint(jax.random.fold_in(jax.random.fold_in(_rk, 2), 6), (1024,), 2, 99999, jnp.int32), jax.random.randint(jax.random.fold_in(jax.random.fold_in(_rk, 2), 7), (1024,), 2, 99995, jnp.int32), jax.random.randint(jax.random.fold_in(jax.random.fold_in(_rk, 2), 8), (1024,), 0, 99999, jnp.int32), jax.random.randint(jax.random.fold_in(jax.random.fold_in(_rk, 2), 9), (1024,), 2, 99986, jnp.int32), jax.random.randint(jax.random.fold_in(jax.random.fold_in(_rk, 2), 10), (1024,), 4, 99999, jnp.int32), jax.random.randint(jax.random.fold_in(jax.random.fold_in(_rk, 2), 11), (1024,), 15, 99999, jnp.int32), jax.random.randint(jax.random.fold_in(jax.random.fold_in(_rk, 2), 12), (1024,), 0, 99989, jnp.int32), jax.random.randint(jax.random.fold_in(jax.random.fold_in(_rk, 2), 13), (1024,), 5, 99990, jnp.int32), jax.random.randint(jax.random.fold_in(jax.random.fold_in(_rk, 2), 14), (1024,), 2, 99996, jnp.int32), jax.random.randint(jax.random.fold_in(jax.random.fold_in(_rk, 2), 15), (1024,), 3, 99994, jnp.int32), jax.random.randint(jax.random.fold_in(jax.random.fold_in(_rk, 2), 16), (1024,), 0, 99998, jnp.int32), jax.random.randint(jax.random.fold_in(jax.random.fold_in(_rk, 2), 17), (1024,), 13, 99998, jnp.int32), jax.random.randint(jax.random.fold_in(jax.random.fold_in(_rk, 2), 18), (1024,), 10, 12498, jnp.int32), jax.random.randint(jax.random.fold_in(jax.random.fold_in(_rk, 2), 19), (1024,), 0, 99999, jnp.int32), jax.random.randint(jax.random.fold_in(jax.random.fold_in(_rk, 2), 20), (1024,), 0, 99995, jnp.int32), jax.random.randint(jax.random.fold_in(jax.random.fold_in(_rk, 2), 21), (1024,), 1, 99998, jnp.int32), jax.random.randint(jax.random.fold_in(jax.random.fold_in(_rk, 2), 22), (1024,), 1, 99997, jnp.int32), jax.random.randint(jax.random.fold_in(jax.random.fold_in(_rk, 2), 23), (1024,), 2, 99989, jnp.int32), jax.random.randint(jax.random.fold_in(jax.random.fold_in(_rk, 2), 24), (1024,), 6, 12500, jnp.int32), jax.random.randint(jax.random.fold_in(jax.random.fold_in(_rk, 2), 25), (1024,), 2, 99995, jnp.int32)], axis=1)
        return (r_x_num, r_x_cat)
    r_x_num, r_x_cat = _rec_inputs()

    def _L0_rec_setup():
        import jax, jax.numpy as jnp
        import numpy as np
        B = 2048
        N_NUM = 13
        N_FIELDS = 26
        VOCAB = 12500
        K = 64
        HIDDEN = [1024, 512, 256]
        DEEP_IN = N_NUM + N_FIELDS * K
        key = jax.random.key(seed)
        ks = jax.random.split(key, 16)
        x_num = jax.random.normal(ks[0], (B, N_NUM), dtype=jnp.float32)
        x_cat = jax.random.randint(ks[1], (B, N_FIELDS), 0, VOCAB, dtype=jnp.int32)
        bias = jnp.zeros((1,), dtype=jnp.float32)
        w_num = jax.random.normal(ks[2], (N_NUM, 1), dtype=jnp.float32) * 0.1
        lin_cat = jax.random.normal(ks[3], (N_FIELDS, VOCAB, 1), dtype=jnp.float32) * 0.01
        v_num = jax.random.normal(ks[4], (N_NUM, K), dtype=jnp.float32) * 0.01
        v_cat = jax.random.normal(ks[5], (N_FIELDS, VOCAB, K), dtype=jnp.float32) * 0.01
        W1 = jax.random.normal(ks[6], (DEEP_IN, HIDDEN[0]), dtype=jnp.float32) * (1.0 / np.sqrt(DEEP_IN))
        b1 = jnp.zeros((HIDDEN[0],), dtype=jnp.float32)
        W2 = jax.random.normal(ks[7], (HIDDEN[0], HIDDEN[1]), dtype=jnp.float32) * (1.0 / np.sqrt(HIDDEN[0]))
        b2 = jnp.zeros((HIDDEN[1],), dtype=jnp.float32)
        W3 = jax.random.normal(ks[8], (HIDDEN[1], HIDDEN[2]), dtype=jnp.float32) * (1.0 / np.sqrt(HIDDEN[1]))
        b3 = jnp.zeros((HIDDEN[2],), dtype=jnp.float32)
        Wo = jax.random.normal(ks[9], (HIDDEN[2], 1), dtype=jnp.float32) * (1.0 / np.sqrt(HIDDEN[2]))
        bo = jnp.zeros((1,), dtype=jnp.float32)
        return {'x_num': x_num, 'x_cat': x_cat, 'bias': bias, 'w_num': w_num, 'lin_cat': lin_cat, 'v_num': v_num, 'v_cat': v_cat, 'W1': W1, 'b1': b1, 'W2': W2, 'b2': b2, 'W3': W3, 'b3': b3, 'Wo': Wo, 'bo': bo}
    _L0_rec_all = _L0_rec_setup()
    _L0_rec_in = {k: v for k, v in _L0_rec_all.items() if k in ('bias', 'w_num', 'lin_cat', 'v_num', 'v_cat', 'W1', 'b1', 'W2', 'b2', 'W3', 'b3', 'Wo', 'bo')}
    del _L0_rec_all
    return {'r_x_num': r_x_num, 'r_x_cat': r_x_cat, 'L0_rec_bias': _L0_rec_in['bias'], 'L0_rec_w_num': _L0_rec_in['w_num'], 'L0_rec_lin_cat': _L0_rec_in['lin_cat'], 'L0_rec_v_num': _L0_rec_in['v_num'], 'L0_rec_v_cat': _L0_rec_in['v_cat'], 'L0_rec_W1': _L0_rec_in['W1'], 'L0_rec_b1': _L0_rec_in['b1'], 'L0_rec_W2': _L0_rec_in['W2'], 'L0_rec_b2': _L0_rec_in['b2'], 'L0_rec_W3': _L0_rec_in['W3'], 'L0_rec_b3': _L0_rec_in['b3'], 'L0_rec_Wo': _L0_rec_in['Wo'], 'L0_rec_bo': _L0_rec_in['bo']}

def reference(r_x_num, r_x_cat, L0_rec_bias, L0_rec_w_num, L0_rec_lin_cat, L0_rec_v_num, L0_rec_v_cat, L0_rec_W1, L0_rec_b1, L0_rec_W2, L0_rec_b2, L0_rec_W3, L0_rec_b3, L0_rec_Wo, L0_rec_bo):
    import jax
    import jax.numpy as jnp

    def _L0_rec_ref(x_num, x_cat, bias, w_num, lin_cat, v_num, v_cat, W1, b1, W2, b2, W3, b3, Wo, bo):
        import jax, jax.numpy as jnp
        import numpy as np
        B = 2048
        N_NUM = 13
        N_FIELDS = 26
        VOCAB = 12500
        K = 64
        HIDDEN = [1024, 512, 256]
        DEEP_IN = N_NUM + N_FIELDS * K
        fid = jnp.arange(N_FIELDS)[None, :]
        lin = bias + x_num @ w_num + lin_cat[fid, x_cat].sum(axis=1)
        vn = x_num[:, :, None] * v_num[None, :, :]
        vc = v_cat[fid, x_cat]
        v = jnp.concatenate([vn, vc], axis=1)
        sum_v = v.sum(axis=1)
        interactions = 0.5 * (sum_v * sum_v - (v * v).sum(axis=1)).sum(axis=1, keepdims=True)
        deep_in = jnp.concatenate([x_num, vc.reshape(vc.shape[0], -1)], axis=1)
        h = jax.nn.relu(deep_in @ W1 + b1)
        h = jax.nn.relu(h @ W2 + b2)
        h = jax.nn.relu(h @ W3 + b3)
        deep_out = h @ Wo + bo
        return lin + interactions + deep_out
    y = _L0_rec_ref(r_x_num, r_x_cat, L0_rec_bias, L0_rec_w_num, L0_rec_lin_cat, L0_rec_v_num, L0_rec_v_cat, L0_rec_W1, L0_rec_b1, L0_rec_W2, L0_rec_b2, L0_rec_W3, L0_rec_b3, L0_rec_Wo, L0_rec_bo)
    return y

_drawn_inputs = setup_inputs


def setup_inputs(seed=0):
    import zlib

    import numpy as np

    out = dict(_drawn_inputs(seed))
    spreads = {'L0_rec_b1': (0.0, 0.1), 'L0_rec_b2': (0.0, 0.1), 'L0_rec_b3': (0.0, 0.1)}
    factors = {}
    for name, (base, spread) in spreads.items():
        noise = np.random.default_rng([zlib.crc32(name.encode()), seed]).standard_normal(out[name].shape)
        drawn = base * np.exp(spread * noise) if base else spread * noise
        out[name] = jnp.asarray(drawn.astype(out[name].dtype))
    for name, factor in factors.items():
        out[name] = (out[name] * factor).astype(out[name].dtype)
    return out
```

```python
from contextlib import ExitStack

import concourse.bass as bass
from concourse import mybir

F32 = mybir.dt.float32
F32R = mybir.dt.float32r
I32 = mybir.dt.int32
ALU = mybir.AluOpType
ACT = mybir.ActivationFunctionType
AX_X = mybir.AxisListType.X

P = 128
BATCH = 1024
TILES = BATCH // P
FIELDS = 26
VOCAB = 12500
K = 64
ROW = K + 1
PAIR = 2 * ROW
N_NUM = 13
H1, H2, H3 = 1024, 512, 256
BANK = 512
HALVES = H1 // BANK

KB = FIELDS // 2
GROUPS = (KB + 1) // 2
BLOCKS = [list(range(2 * g, min(2 * g + 2, KB))) for g in range(GROUPS)]
EARLY = KB - len(BLOCKS[-1])

PART = 32
NUM_K = 3 * PART
C_B2 = H1
C_B3 = C_B2 + H2
C_FM = C_B3 + H3
FM_COLS = ROW + 1
NUM_COLS = C_FM + FM_COLS
Z_FM = H3
Z_SQ = Z_FM + FM_COLS

RAW_SLOTS = 4
NUM_SLOTS = -(-NUM_COLS // H1)
W2_CHUNK = H1 // H2
W2_CHUNKS = (H1 // P) // W2_CHUNK
CHUNKS = KB + W2_CHUNKS + 1
GATHERED = 16


def deepfm(nc, table, x_cat, x_num, w_num, W1, W2, W3, Wo, out):
    with ExitStack() as ctx:
        def sb(name, shape, dt=F32):
            return ctx.enter_context(nc.sbuf_tensor(name, shape, dt))

        def sem(name):
            return ctx.enter_context(nc.semaphore(name))

        raw = sb("raw", [P, RAW_SLOTS * H1])
        w1_hi = sb("w1_hi", [P, KB, H1], F32R)
        w1_lo = sb("w1_lo", [P, KB, H1], F32R)
        w2_hi = sb("w2_hi", [P, H1 // P, H2], F32R)
        w2_lo = sb("w2_lo", [P, H1 // P, H2], F32R)
        w3_hi = sb("w3_hi", [P, H2 // P, H3], F32R)
        w3_lo = sb("w3_lo", [P, H2 // P, H3], F32R)
        wnum = sb("wnum", [NUM_K, NUM_COLS], F32R)
        wo_all = sb("wo_all", [P, H3])
        vnum_sq = sb("vnum_sq", [PART, 1])
        ident = sb("ident", [P, P])
        cat = sb("cat", [P, TILES * FIELDS], I32)
        wrap = sb("wrap", [P, TILES * FIELDS], I32)
        first_row = sb("first_row", [P, TILES * FIELDS], I32)
        rows = [sb(f"rows{p}", [P, FIELDS], I32) for p in range(2)]
        emb = [sb(f"emb{p}", [P, FIELDS * ROW]) for p in range(2)]
        xnum = [sb(f"xnum{p}", [NUM_K, P]) for p in range(2)]
        xnum_r = [sb(f"xnum_r{p}", [NUM_K, P], F32R) for p in range(2)]
        xnum_sq = [sb(f"xnum_sq{p}", [PART, P]) for p in range(2)]
        x_hi = [sb(f"x_hi{s}", [P, 2 * P], F32R) for s in range(2)]
        x_lo = [sb(f"x_lo{s}", [P, 2 * P], F32R) for s in range(2)]
        h1 = sb("h1", [P, H1])
        h2 = sb("h2", [P, H2])
        hT_hi = [sb(f"hT_hi{s}", [P, BANK], F32R) for s in range(2)]
        hT_lo = [sb(f"hT_lo{s}", [P, BANK], F32R) for s in range(2)]
        pair_sum = sb("pair_sum", [P, PAIR])
        emb_sum = [sb(f"emb_sum{p}", [P, ROW]) for p in range(2)]
        emb_sq = [sb(f"emb_sq{p}", [P, 2]) for p in range(2)]
        total = sb("total", [P, ROW])
        score = sb("score", [P, 4])
        y = sb("y", [P, TILES])
        sq_out = raw[:, 0:FIELDS * K]
        deep_out = raw[:, 2 * H1:2 * H1 + H3]
        ssq_out = raw[:, 3 * H1:3 * H1 + K]

        acc = [[ctx.enter_context(nc.psum_tensor(f"acc{p}{h}", [P, BANK], F32)) for h in range(HALVES)]
               for p in range(2)]
        xT = [ctx.enter_context(nc.psum_tensor(f"xT{s}", [P, BANK], F32)) for s in range(2)]
        hT = ctx.enter_context(nc.psum_tensor("hT", [P, BANK], F32))
        Z = ctx.enter_context(nc.psum_tensor("Z", [P, BANK], F32))

        cat_loaded = sem("cat_loaded")
        wnum_loaded = sem("wnum_loaded")
        wo_loaded = sem("wo_loaded")
        chunk_loaded = [sem(f"chunk_loaded{s}") for s in range(RAW_SLOTS)]
        xnum_loaded = [sem(f"xnum_loaded{p}") for p in range(2)]
        gathered = [[sem(f"gathered{p}{g}") for g in range(GROUPS)] for p in range(2)]
        gather_open = sem("gather_open")
        stored = sem("stored")
        first_row_ready = sem("first_row_ready")
        ident_zero = sem("ident_zero")
        ident_ready = sem("ident_ready")
        rows_step = sem("rows_step")
        rows_ready = sem("rows_ready")
        wnum_round = sem("wnum_round")
        wnum_ready = sem("wnum_ready")
        vnum_sq_ready = sem("vnum_sq_ready")
        w_hi_ready = sem("w_hi_ready")
        w_lo_ready = sem("w_lo_ready")
        xnum_round = sem("xnum_round")
        xnum_ready = sem("xnum_ready")
        x_turned = sem("x_turned")
        x_hi_ready = sem("x_hi_ready")
        x_lo_ready = sem("x_lo_ready")
        x_used = sem("x_used")
        acc_done = [sem(f"acc_done{h}") for h in range(HALVES)]
        relu1_done = [sem(f"relu1_done{h}") for h in range(HALVES)]
        h_turned = sem("h_turned")
        h_hi_ready = sem("h_hi_ready")
        h_lo_ready = sem("h_lo_ready")
        l2_done = sem("l2_done")
        relu2_done = sem("relu2_done")
        l3_done = sem("l3_done")
        z_read = sem("z_read")
        sum_early = sem("sum_early")
        sum_pairs = sem("sum_pairs")
        sum_done = sem("sum_done")
        sq_done = sem("sq_done")
        score_step = sem("score_step")
        y_ready = sem("y_ready")

        def slot(p, g):
            return (p * GROUPS + g) % 2

        def group_no(t, g):
            return t * GROUPS + g

        def pairs(p, k0, k1):
            return emb[p][:, :].rearrange("b (k e) -> b k e", e=PAIR)[:, k0:k1, :]

        def chunk_slot(j):
            return (NUM_SLOTS + j) % RAW_SLOTS

        def chunk_raw(j):
            return raw[:, chunk_slot(j) * H1:(chunk_slot(j) + 1) * H1]

        def chunk_split(j):
            if j < KB:
                return w1_hi[:, j, :], w1_lo[:, j, :]
            if j < KB + W2_CHUNKS:
                b = (j - KB) * W2_CHUNK
                return [w[:, b:b + W2_CHUNK, :].rearrange("p b n -> p (b n)") for w in (w2_hi, w2_lo)]
            return [w[:, :, :].rearrange("p b n -> p (b n)") for w in (w3_hi, w3_lo)]

        block = ctx.enter_context(nc.Block())

        @block.sync
        def _(sp):
            sp.dma_start(cat[:, :], x_cat).then_inc(cat_loaded, 16)
            sp.dma_start(raw[0:NUM_K, 0:NUM_COLS], w_num).then_inc(wnum_loaded, 16)

            def load_xnum(t, p):
                sp.dma_start(xnum[p][:, :], x_num[:, bass.ds(t * P, P)]).then_inc(xnum_loaded[p], 16)

            load_xnum(0, 0)
            load_xnum(1, 1)
            for j in range(CHUNKS):
                if j == RAW_SLOTS - NUM_SLOTS:
                    sp.wait_ge(wnum_ready, 1)
                if j >= RAW_SLOTS:
                    sp.wait_ge(w_lo_ready, j - RAW_SLOTS + 1)
                if j < KB:
                    src = W1[j * P:(j + 1) * P, :]
                    dst = chunk_raw(j)
                elif j < KB + W2_CHUNKS:
                    b = (j - KB) * W2_CHUNK
                    src = W2.rearrange("(b p) n -> p b n", p=P)[:, b:b + W2_CHUNK, :]
                    dst = chunk_raw(j).rearrange("p (b n) -> p b n", n=H2)
                else:
                    src = W3.rearrange("(b p) n -> p b n", p=P)
                    dst = chunk_raw(j).rearrange("p (b n) -> p b n", n=H3)
                sp.dma_start(dst, src).then_inc(chunk_loaded[chunk_slot(j)], 16)
            sp.dma_start(wo_all[:, :], Wo.to_broadcast((P, H3))).then_inc(wo_loaded, 16)
            with sp.Fori(0, (TILES - 2) // 2) as i:
                for p in range(2):
                    sp.wait_ge(xnum_ready, 2 * i + p + 1)
                    load_xnum(2 * i + p + 2, p)
            sp.wait_ge(y_ready, TILES)
            sp.dma_start(out, y[:, :]).then_inc(stored, 16)
            sp.wait_ge(stored, 16)

        @block.gpsimd
        def _(pool):
            pool.iota(first_row[:, :].rearrange("p (t f) -> p t f", f=FIELDS),
                      pattern=[[0, TILES], [VOCAB, FIELDS]], base=0, channel_multiplier=0).then_inc(first_row_ready, 1)
            pool.memset(ident[:, :], 0.0).then_inc(ident_zero, 1)
            pool.wait_ge(ident_zero, 1)
            pool.affine_select(out=ident[:, :], in_=ident[:, :], compare_op=ALU.not_equal, fill=1.0, base=0,
                               pattern=[[-1, P]], channel_multiplier=1).then_inc(ident_ready, 1)

            def gather(t, p):
                pool.wait_ge(rows_ready, t + 1)
                pool.sem_inc(gather_open, 1)
                for f in range(FIELDS):
                    pool.indirect_dma_start(
                        emb[p][:, f * ROW:(f + 1) * ROW], None, table,
                        bass.IndirectOffsetOnAxis(ap=rows[p][:, f:f + 1], axis=0),
                    ).then_inc(gathered[p][f // 4], GATHERED)

            gather(0, 0)
            gather(1, 1)
            with pool.Fori(0, (TILES - 2) // 2) as i:
                for p in range(2):
                    pool.wait_ge(x_turned, group_no(2 * i + p + 1, 0))
                    pool.wait_ge(sum_done, 2 * i + p + 1)
                    pool.wait_ge(sq_done, 2 * i + p + 1)
                    gather(2 * i + p + 2, p)

        @block.tensor
        def _(pe):
            def turn_x(t, p, g, use):
                pe.wait_ge(gathered[p][g], 2 * len(BLOCKS[g]) * GATHERED * use)
                for n, k in enumerate(BLOCKS[g]):
                    mm = pe.transpose(xT[slot(p, g)][:, n * P:(n + 1) * P], pairs(p, k, k + 1)[:, 0, 1:1 + P],
                                      ident[:, :])
                mm.then_inc(x_turned, 1)

            def layer1_num(t, p):
                pe.wait_ge(xnum_ready, t + 1)
                for h in range(HALVES):
                    pe.matmul(acc[p][h][:, :], xnum_r[p][:, :], wnum[:, h * BANK:(h + 1) * BANK],
                              start=True, stop=False)

            def layer1(t, p, g, first):
                s, last = slot(p, g), g == GROUPS - 1
                pe.wait_ge(x_hi_ready, group_no(t, g) + 1)
                for h in range(HALVES):
                    cols = slice(h * BANK, (h + 1) * BANK)
                    for n, k in enumerate(BLOCKS[g]):
                        if first and h == 0:
                            pe.wait_ge(w_lo_ready, k + 1)
                        xh = x_hi[s][:, n * P:(n + 1) * P]
                        pe.matmul(acc[p][h][:, :], xh, w1_hi[:, k, cols], start=False, stop=False)
                        pe.matmul(acc[p][h][:, :], xh, w1_lo[:, k, cols], start=False, stop=False)
                    if h == 0:
                        pe.wait_ge(x_lo_ready, group_no(t, g) + 1)
                    for n, k in enumerate(BLOCKS[g]):
                        mm = pe.matmul(acc[p][h][:, :], x_lo[s][:, n * P:(n + 1) * P], w1_hi[:, k, cols],
                                       start=False, stop=last and k == BLOCKS[g][-1])
                    if last:
                        mm.then_inc(acc_done[h], 1)
                if not last:
                    mm.then_inc(x_used, 1)

            def turn_h1(t, half, bank):
                pe.wait_ge(relu1_done[half], t + 1)
                for n in range(BANK // P):
                    mm = pe.transpose(bank[:, n * P:(n + 1) * P], h1[:, half * BANK + n * P:half * BANK + (n + 1) * P],
                                      ident[:, :])
                mm.then_inc(h_turned, 1)

            def layer2_bias(t, p, first):
                if not first:
                    pe.wait_ge(z_read, t)
                pe.matmul(Z[:, 0:H2], xnum_r[p][:, :], wnum[:, C_B2:C_B2 + H2], start=True, stop=False)

            def layer2(t, ks):
                for k in ks:
                    half, n = divmod(k, BANK // P)
                    if n == 0 or k == ks[0]:
                        pe.wait_ge(h_lo_ready, 3 * t + half + 1)
                    hh, hl = (h[half][:, n * P:(n + 1) * P] for h in (hT_hi, hT_lo))
                    pe.matmul(Z[:, 0:H2], hh, w2_hi[:, k, :], start=False, stop=False)
                    pe.matmul(Z[:, 0:H2], hh, w2_lo[:, k, :], start=False, stop=False)
                    mm = pe.matmul(Z[:, 0:H2], hl, w2_hi[:, k, :], start=False, stop=(k == H1 // P - 1))
                if ks[-1] == H1 // P - 1:
                    mm.then_inc(l2_done, 1)

            def turn_h2(t, bank):
                pe.wait_ge(relu2_done, t + 1)
                for n in range(H2 // P):
                    mm = pe.transpose(bank[:, n * P:(n + 1) * P], h2[:, n * P:(n + 1) * P], ident[:, :])
                mm.then_inc(h_turned, 1)

            def layer3_and_fm(t, p):
                pe.matmul(Z[:, 0:H3], xnum_r[p][:, :], wnum[:, C_B3:C_B3 + H3], start=True, stop=False)
                pe.wait_ge(h_lo_ready, 3 * t + 3)
                for k in range(H2 // P):
                    hh, hl = (h[0][:, k * P:(k + 1) * P] for h in (hT_hi, hT_lo))
                    pe.matmul(Z[:, 0:H3], hh, w3_hi[:, k, :], start=False, stop=False)
                    pe.matmul(Z[:, 0:H3], hh, w3_lo[:, k, :], start=False, stop=False)
                    pe.matmul(Z[:, 0:H3], hl, w3_hi[:, k, :], start=False, stop=(k == H2 // P - 1))
                pe.matmul(Z[:, Z_FM:Z_FM + FM_COLS], xnum_r[p][:, :], wnum[:, C_FM:C_FM + FM_COLS],
                          start=True, stop=True)
                pe.matmul(Z[:, Z_SQ:Z_SQ + 1], xnum_sq[p][:, :], vnum_sq[:, :],
                          start=True, stop=True).then_inc(l3_done, 1)

            def tile(t, p, use, first=False, second=False):
                for g in range(GROUPS):
                    turn_x(t, p, g, use)
                    if g == 0:
                        layer1_num(t, p)
                    if not first:
                        if g == 1:
                            turn_h1(t - 1, 0, hT)
                        if g == 2:
                            pe.wait_ge(h_lo_ready, 3 * (t - 1) + 1)
                            turn_h1(t - 1, 1, hT)
                            if second:
                                pe.wait_ge(w_lo_ready, CHUNKS)
                            layer2_bias(t - 1, 1 - p, second)
                            layer2(t - 1, [0, 1])
                        if g == 3:
                            layer2(t - 1, [2, 3, 4])
                        if g == 4:
                            layer2(t - 1, [5, 6, 7])
                        if g == 5:
                            turn_h2(t - 1, hT)
                        if g == 6:
                            layer3_and_fm(t - 1, 1 - p)
                    layer1(t, p, g, first)

            pe.wait_ge(ident_ready, 1)
            pe.wait_ge(wnum_ready, 1)
            pe.wait_ge(vnum_sq_ready, 1)
            tile(0, 0, 1, first=True)
            tile(1, 1, 1, second=True)
            with pe.Fori(0, (TILES - 2) // 2) as i:
                for p in range(2):
                    tile(2 * i + p + 2, p, i + 2)
            t, p = TILES - 1, (TILES - 1) % 2
            turn_h1(t, 0, hT)
            turn_h1(t, 1, xT[0])
            layer2_bias(t, p, False)
            layer2(t, list(range(H1 // P)))
            turn_h2(t, xT[1])
            layer3_and_fm(t, p)

        @block.scalar
        def _(act):
            def split_hi(j):
                act.wait_ge(chunk_loaded[chunk_slot(j)], 16 * chunk_round(j))
                act.activation(chunk_split(j)[0], chunk_raw(j), ACT.Copy).then_inc(w_hi_ready, 1)

            def chunk_round(j):
                return sum(1 for i in range(j + 1) if chunk_slot(i) == chunk_slot(j))

            def x_part(t, p, g, first=False):
                s, n = slot(p, g), len(BLOCKS[g]) * P
                act.wait_ge(x_turned, group_no(t, g) + 1)
                if g >= 2:
                    act.wait_ge(x_used, x_uses(t, g - 2))
                elif not first:
                    if g == 0:
                        act.wait_ge(x_used, x_uses(t - 1, GROUPS - 2))
                    else:
                        act.wait_ge(acc_done[1], t)
                act.activation(x_hi[s][:, 0:n], xT[s][:, 0:n], ACT.Copy).then_inc(x_hi_ready, 1)

            def x_uses(t, g):
                return t * (GROUPS - 1) + g + 1

            def relu1(t, p):
                act.wait_ge(acc_done[0], t + 1)
                act.activation(h1[:, 0:BANK], acc[p][0][:, :], ACT.Relu).then_inc(relu1_done[0], 1)

            def h_part(t, n, bank, s):
                act.wait_ge(h_turned, 3 * t + n + 1)
                act.activation(hT_hi[s][:, :], bank[:, :], ACT.Copy).then_inc(h_hi_ready, 1)

            def relu2(t):
                act.wait_ge(l2_done, t + 1)
                act.activation(h2[:, :], Z[:, 0:H2], ACT.Relu).then_inc(relu2_done, 1)

            def squares(p, n):
                k0, k1 = [(0, EARLY), (EARLY, KB)][n]
                op = act.activation(sq_out[:, k0 * P:k1 * P].rearrange("b (k e) -> b k e", e=P),
                                    pairs(p, k0, k1)[:, :, 1:1 + P], ACT.Square, accum_out=emb_sq[p][:, n:n + 1])
                if n == 1:
                    op.then_inc(sq_done, 1)

            def tile(t, p):
                x_part(t, p, 0)
                relu1(t - 1, 1 - p)
                x_part(t, p, 1)
                h_part(t - 1, 0, hT, 0)
                x_part(t, p, 2)
                h_part(t - 1, 1, hT, 1)
                x_part(t, p, 3)
                x_part(t, p, 4)
                relu2(t - 1)
                x_part(t, p, 5)
                h_part(t - 1, 2, hT, 0)
                squares_wait(t)
                squares(p, 0)
                x_part(t, p, 6)
                squares(p, 1)

            def squares_wait(t):
                act.wait_ge(y_ready, t - 1)

            for g in range(GROUPS):
                for k in BLOCKS[g]:
                    split_hi(k)
                x_part(0, 0, g, first=True)
            for j in range(KB, CHUNKS):
                split_hi(j)
            act.wait_ge(w_lo_ready, CHUNKS)
            squares(0, 0)
            squares(0, 1)
            x_part(1, 1, 0)
            relu1(0, 0)
            x_part(1, 1, 1)
            h_part(0, 0, hT, 0)
            x_part(1, 1, 2)
            h_part(0, 1, hT, 1)
            x_part(1, 1, 3)
            x_part(1, 1, 4)
            relu2(0)
            x_part(1, 1, 5)
            h_part(0, 2, hT, 0)
            squares(1, 0)
            x_part(1, 1, 6)
            squares(1, 1)
            with act.Fori(0, (TILES - 2) // 2) as i:
                for p in range(2):
                    tile(2 * i + p + 2, p)
            t, p = TILES - 1, (TILES - 1) % 2
            relu1(t, p)
            h_part(t, 0, hT, 0)
            h_part(t, 1, xT[0], 1)
            relu2(t)
            h_part(t, 2, xT[1], 0)

        @block.vector
        def _(dve):
            def row_numbers(a, b, n):
                dve.tensor_scalar(wrap[:, a:b], cat[:, a:b], 0.0, float(VOCAB), ALU.is_lt, ALU.mult).then_inc(rows_step, 1)
                dve.wait_ge(rows_step, 3 * n + 1)
                dve.tensor_tensor(cat[:, a:b], cat[:, a:b], wrap[:, a:b], ALU.add).then_inc(rows_step, 1)
                dve.wait_ge(rows_step, 3 * n + 2)
                dve.tensor_scalar(cat[:, a:b], cat[:, a:b], 0.0, float(VOCAB - 1), ALU.max, ALU.min).then_inc(rows_step, 1)
                dve.wait_ge(rows_step, 3 * n + 3)

            def split_wnum():
                dve.wait_ge(wnum_loaded, 16)
                dve.tensor_copy(wnum[:, :], raw[0:NUM_K, 0:NUM_COLS]).then_inc(wnum_round, 1)
                dve.scalar_tensor_tensor(out=total[0:PART, 0:K], in0=raw[0:PART, C_FM:C_FM + K], scalar=1.0,
                                         in1=raw[0:PART, C_FM:C_FM + K], op0=ALU.mult, op1=ALU.mult,
                                         accum_out=vnum_sq[:, :]).then_inc(vnum_sq_ready, 1)
                dve.wait_ge(wnum_round, 1)
                dve.tensor_tensor(wnum[2 * PART:NUM_K, :], raw[2 * PART:NUM_K, 0:NUM_COLS],
                                  wnum[2 * PART:NUM_K, :].bitcast(F32), ALU.subtract).then_inc(wnum_ready, 1)

            def split_xnum(t, p, use):
                dve.wait_ge(xnum_loaded[p], 16 * use)
                dve.tensor_copy(xnum_r[p][:, :], xnum[p][:, :]).then_inc(xnum_round, 1)
                dve.tensor_tensor(xnum_sq[p][:, :], xnum[p][0:PART, :], xnum[p][0:PART, :], ALU.mult)
                dve.wait_ge(xnum_round, t + 1)
                dve.tensor_tensor(xnum_r[p][PART:2 * PART, :], xnum[p][PART:2 * PART, :],
                                  xnum_r[p][PART:2 * PART, :].bitcast(F32), ALU.subtract).then_inc(xnum_ready, 1)

            def split_lo(j):
                hi, lo = chunk_split(j)
                dve.wait_ge(w_hi_ready, j + 1)
                dve.tensor_tensor(lo, chunk_raw(j), hi.bitcast(F32), ALU.subtract).then_inc(w_lo_ready, 1)

            def take_rows(t, p):
                dve.tensor_copy(rows[p][:, :], cat[:, bass.ds(t * FIELDS, FIELDS)]).then_inc(rows_ready, 1)

            def x_part(t, p, g):
                s, n = slot(p, g), len(BLOCKS[g]) * P
                dve.wait_ge(x_hi_ready, group_no(t, g) + 1)
                dve.tensor_tensor(x_lo[s][:, 0:n], xT[s][:, 0:n], x_hi[s][:, 0:n].bitcast(F32),
                                  ALU.subtract).then_inc(x_lo_ready, 1)

            def relu1(t, p):
                dve.wait_ge(acc_done[1], t + 1)
                dve.tensor_scalar(h1[:, BANK:H1], acc[p][1][:, :], 0.0, None, ALU.max).then_inc(relu1_done[1], 1)

            def h_part(t, n, bank, s):
                dve.wait_ge(h_hi_ready, 3 * t + n + 1)
                dve.tensor_tensor(hT_lo[s][:, :], bank[:, :], hT_hi[s][:, :].bitcast(F32),
                                  ALU.subtract).then_inc(h_lo_ready, 1)

            def sum_most(p):
                dve.tensor_reduce(pair_sum[:, :], pairs(p, 0, EARLY).rearrange("b k e -> b e k"), AX_X,
                                  ALU.add).then_inc(sum_early, 1)

            def sum_rest(t, p):
                dve.wait_ge(sum_early, t + 1)
                dve.tensor_tensor(pair_sum[:, :], pair_sum[:, :], pairs(p, KB - 1, KB)[:, 0, :],
                                  ALU.add).then_inc(sum_pairs, 1)
                dve.wait_ge(sum_pairs, t + 1)
                dve.tensor_tensor(emb_sum[p][:, 0:K], pair_sum[:, 1:1 + K], pair_sum[:, 1 + K:1 + 2 * K], ALU.add)
                dve.tensor_tensor(emb_sum[p][:, K:ROW], pair_sum[:, 0:1], pair_sum[:, PAIR - 1:PAIR],
                                  ALU.add).then_inc(sum_done, 1)

            def scores(t, p):
                dve.wait_ge(l3_done, t + 1)
                dve.wait_ge(sq_done, t + 1)
                dve.wait_ge(sum_done, t + 1)
                dve.tensor_tensor(total[:, :], emb_sum[p][:, :], Z[:, Z_FM:Z_FM + ROW], ALU.add).then_inc(score_step, 1)
                dve.scalar_tensor_tensor(out=deep_out, in0=Z[:, 0:H3], scalar=0.0, in1=wo_all[:, :], op0=ALU.max,
                                         op1=ALU.mult, accum_out=score[:, 1:2]).then_inc(score_step, 1)
                dve.scalar_tensor_tensor(out=score[:, 2:3], in0=Z[:, Z_SQ:Z_SQ + 1], scalar=emb_sq[p][:, 0:1],
                                         in1=emb_sq[p][:, 1:2], op0=ALU.add, op1=ALU.add).then_inc(z_read, 1)
                dve.wait_ge(score_step, 4 * t + 1)
                dve.scalar_tensor_tensor(out=ssq_out, in0=total[:, 0:K], scalar=1.0, in1=total[:, 0:K], op0=ALU.mult,
                                         op1=ALU.mult, accum_out=score[:, 0:1]).then_inc(score_step, 1)
                dve.wait_ge(z_read, t + 1)
                dve.wait_ge(score_step, 4 * t + 3)
                dve.tensor_scalar(score[:, 3:4], score[:, 0:1], score[:, 2:3], 0.5, ALU.subtract,
                                  ALU.mult).then_inc(score_step, 1)
                dve.wait_ge(score_step, 4 * t + 4)
                dve.scalar_tensor_tensor(out=y[:, bass.ds(t, 1)], in0=score[:, 3:4], scalar=total[:, K:ROW],
                                         in1=score[:, 1:2], op0=ALU.add, op1=ALU.add).then_inc(y_ready, 1)

            def tile(t, p, use, before_last=True):
                if before_last is not False:
                    take_rows_if(t, p, before_last)
                x_part(t, p, 0)
                relu1(t - 1, 1 - p)
                x_part(t, p, 1)
                h_part(t - 1, 0, hT, 0)
                x_part(t, p, 2)
                h_part(t - 1, 1, hT, 1)
                x_part(t, p, 3)
                x_part(t, p, 4)
                x_part(t, p, 5)
                h_part(t - 1, 2, hT, 0)
                sum_most(p)
                x_part(t, p, 6)
                sum_rest(t, p)

            def take_rows_if(t, p, yes):
                take_rows(t + 1, 1 - p)

            def tile_end(t, p, use, last=False):
                if not last:
                    dve.wait_ge(l3_done, t)
                    split_xnum(t + 1, 1 - p, use)
                scores(t - 1, 1 - p)

            dve.wait_ge(cat_loaded, 16)
            dve.wait_ge(first_row_ready, 1)
            row_numbers(0, FIELDS, 0)
            dve.tensor_tensor(rows[0][:, :], cat[:, 0:FIELDS], first_row[:, 0:FIELDS], ALU.add).then_inc(rows_ready, 1)
            row_numbers(FIELDS, TILES * FIELDS, 1)
            dve.tensor_tensor(cat[:, FIELDS:], cat[:, FIELDS:], first_row[:, FIELDS:], ALU.add).then_inc(rows_step, 1)
            dve.wait_ge(rows_step, 7)
            take_rows(1, 1)
            split_wnum()
            split_xnum(0, 0, 1)
            for g in range(GROUPS):
                for k in BLOCKS[g]:
                    split_lo(k)
                x_part(0, 0, g)
            split_xnum(1, 1, 1)
            for j in range(KB, CHUNKS):
                split_lo(j)
            sum_most(0)
            sum_rest(0, 0)
            dve.wait_ge(wo_loaded, 16)
            tile(1, 1, 1)
            tile_end(1, 1, 2)
            with dve.Fori(0, (TILES - 4) // 2) as i:
                for p in range(2):
                    tile(2 * i + p + 2, p, 0)
                    tile_end(2 * i + p + 2, p, i + 2 + p)
            tile(TILES - 2, 0, 0)
            tile_end(TILES - 2, 0, TILES // 2)
            tile(TILES - 1, 1, 0, before_last=False)
            tile_end(TILES - 1, 1, 0, last=True)
            t, p = TILES - 1, (TILES - 1) % 2
            relu1(t, p)
            h_part(t, 0, hT, 0)
            h_part(t, 1, xT[0], 1)
            h_part(t, 2, xT[1], 0)
            scores(t, p)


def kernel(r_x_num, r_x_cat, L0_rec_bias, L0_rec_w_num, L0_rec_lin_cat, L0_rec_v_num, L0_rec_v_cat, L0_rec_W1,
           L0_rec_b1, L0_rec_W2, L0_rec_b2, L0_rec_W3, L0_rec_b3, L0_rec_Wo, L0_rec_bo):
    import numpy as np
    import concourse.bacc as bacc
    from concourse.bass_utils import run_bass_kernel_spmd as run

    table = np.empty((FIELDS, VOCAB, ROW), np.float32)
    table[0::2, :, 0:1], table[0::2, :, 1:] = np.asarray(L0_rec_lin_cat)[0::2], np.asarray(L0_rec_v_cat)[0::2]
    table[1::2, :, :K], table[1::2, :, K:] = np.asarray(L0_rec_v_cat)[1::2], np.asarray(L0_rec_lin_cat)[1::2]
    table = table.reshape(FIELDS * VOCAB, ROW)
    x_part = np.zeros((PART, BATCH), np.float32)
    x_part[:N_NUM] = np.asarray(r_x_num).reshape(P, TILES, N_NUM).transpose(2, 1, 0).reshape(N_NUM, BATCH)
    x_part[N_NUM:N_NUM + 2] = 1.0
    w_part = np.zeros((PART, NUM_COLS), np.float32)
    w_part[:N_NUM, :H1] = np.asarray(L0_rec_W1)[:N_NUM]
    w_part[N_NUM, :H1] = np.asarray(L0_rec_b1)
    w_part[N_NUM, C_B2:C_B2 + H2] = np.asarray(L0_rec_b2)
    w_part[N_NUM, C_B3:C_B3 + H3] = np.asarray(L0_rec_b3)
    w_part[:N_NUM, C_FM:C_FM + K] = np.asarray(L0_rec_v_num)
    w_part[:N_NUM, C_FM + K] = np.asarray(L0_rec_w_num)[:, 0]
    w_part[N_NUM, C_FM + K] = np.asarray(L0_rec_bias)[0]
    w_part[N_NUM + 1, C_FM + K] = np.asarray(L0_rec_bo)[0]
    arrays = {
        "table": table,
        "x_cat": np.asarray(r_x_cat).reshape(P, TILES * FIELDS),
        "x_num": np.concatenate([x_part] * 3),
        "w_num": np.concatenate([w_part] * 3),
        "W1": np.asarray(L0_rec_W1)[N_NUM:],
        "W2": np.asarray(L0_rec_W2),
        "W3": np.asarray(L0_rec_W3),
        "Wo": np.asarray(L0_rec_Wo).reshape(1, H3),
    }
    nc = bacc.Bacc("TRN2", target_bir_lowering=False, num_devices=1)
    arrays = {f"in_{name}": np.ascontiguousarray(a) for name, a in arrays.items()}
    args = [nc.dram_tensor(name, a.shape, mybir.dt.from_np(a.dtype), kind="ExternalInput").ap()
            for name, a in arrays.items()]
    out = nc.dram_tensor("out", (P, TILES), F32, kind="ExternalOutput").ap()
    deepfm(nc, *args, out)
    return run(nc, [arrays], core_ids=[0]).results[0]["out"].reshape(BATCH, 1)
```

```python
from contextlib import ExitStack

import concourse.bass as bass
from concourse import mybir

F32 = mybir.dt.float32
F32R = mybir.dt.float32r
I32 = mybir.dt.int32
ALU = mybir.AluOpType
ACT = mybir.ActivationFunctionType
AX_X = mybir.AxisListType.X

P = 128
BATCH = 1024
TILES = BATCH // P
FIELDS = 26
VOCAB = 12500
K = 64
ROW = K + 1
PAIR = 2 * ROW
N_NUM = 13
H1, H2, H3 = 1024, 512, 256
BANK = 512
HALVES = H1 // BANK

KB = FIELDS // 2
GROUPS = (KB + 1) // 2
BLOCKS = [list(range(2 * g, min(2 * g + 2, KB))) for g in range(GROUPS)]
EARLY = KB - len(BLOCKS[-1])

PART = 32
NUM_K = 3 * PART
C_FM = H1
FM_COLS = ROW + 1
NUM_COLS = C_FM + FM_COLS
Z_FM = H3
Z_SQ = Z_FM + FM_COLS

RAW_SLOTS = 4
W2_CHUNK = H1 // H2
W2_CHUNKS = (H1 // P) // W2_CHUNK
CHUNKS = KB + W2_CHUNKS + 1
IN_FLIGHT = 2
SPLIT_BEFORE = [3, 5, 8, 10, 12, 14, 15, 15, 16, 17, 18]
GATHERED = 16



def deepfm(nc, table, x_cat, x_num, w_num, W1, W2, W3, vectors, out):
    with ExitStack() as ctx:
        def sb(name, shape, dt=F32):
            return ctx.enter_context(nc.sbuf_tensor(name, shape, dt))

        def sem(name):
            return ctx.enter_context(nc.semaphore(name))

        raw = sb("raw", [P, RAW_SLOTS * H1])
        w1_hi = sb("w1_hi", [P, KB, H1], F32R)
        w1_lo = sb("w1_lo", [P, KB, H1], F32R)
        w2_hi = sb("w2_hi", [P, H1 // P, H2], F32R)
        w2_lo = sb("w2_lo", [P, H1 // P, H2], F32R)
        w3_hi = sb("w3_hi", [P, H2 // P, H3], F32R)
        w3_lo = sb("w3_lo", [P, H2 // P, H3], F32R)
        wnum = sb("wnum", [NUM_K, NUM_COLS], F32R)
        vectors_all = sb("vectors_all", [P, H2 + 2 * H3])
        b2, b3, wo = (vectors_all[:, a:b] for a, b in ((0, H2), (H2, H2 + H3), (H2 + H3, H2 + 2 * H3)))
        vnum_sq = sb("vnum_sq", [PART, 1])
        ident = sb("ident", [P, P])
        cat = sb("cat", [P, TILES * FIELDS], I32)
        wrap = sb("wrap", [P, TILES * FIELDS], I32)
        first_row = sb("first_row", [P, TILES * FIELDS], I32)
        rows = [sb(f"rows{p}", [P, FIELDS], I32) for p in range(2)]
        emb = [sb(f"emb{p}", [P, FIELDS * ROW]) for p in range(2)]
        xnum = [sb(f"xnum{p}", [NUM_K, P]) for p in range(2)]
        xnum_r = [sb(f"xnum_r{p}", [NUM_K, P], F32R) for p in range(2)]
        xnum_sq = [sb(f"xnum_sq{p}", [PART, P]) for p in range(2)]
        x_hi = [sb(f"x_hi{s}", [P, 2 * P], F32R) for s in range(2)]
        x_lo = [sb(f"x_lo{s}", [P, 2 * P], F32R) for s in range(2)]
        h = sb("h", [P, H1 + H2])
        h1, h2 = h[:, 0:H1], h[:, H1:]
        hT_hi = [sb(f"hT_hi{s}", [P, BANK], F32R) for s in range(2)]
        hT_lo = [sb(f"hT_lo{s}", [P, BANK], F32R) for s in range(2)]
        pair_sum = sb("pair_sum", [P, PAIR])
        emb_sum = [sb(f"emb_sum{p}", [P, ROW]) for p in range(2)]
        emb_sq = [sb(f"emb_sq{p}", [P, 2]) for p in range(2)]
        total = sb("total", [P, ROW])
        score = sb("score", [P, 4])
        y = sb("y", [P, TILES])
        wnum_raw = emb[1][0:NUM_K, 0:NUM_COLS]
        sq_out_0 = [h[:, :], hT_hi[0][:, 0:P]]
        sq_out = [raw[:, 0:EARLY * P], raw[:, EARLY * P:KB * P]]
        deep_in = raw[:, 2 * H1:2 * H1 + H3]
        deep_out = raw[:, 2 * H1 + H3:2 * H1 + 2 * H3]
        ssq_out = raw[:, 3 * H1:3 * H1 + K]

        acc = [[ctx.enter_context(nc.psum_tensor(f"acc{p}{h}", [P, BANK], F32)) for h in range(HALVES)]
               for p in range(2)]
        xT = [ctx.enter_context(nc.psum_tensor(f"xT{s}", [P, BANK], F32)) for s in range(2)]
        hT = ctx.enter_context(nc.psum_tensor("hT", [P, BANK], F32))
        Z = ctx.enter_context(nc.psum_tensor("Z", [P, BANK], F32))

        cat_loaded = sem("cat_loaded")
        wnum_loaded = sem("wnum_loaded")
        vectors_loaded = sem("vectors_loaded")
        chunk_loaded = [sem(f"chunk_loaded{s}") for s in range(RAW_SLOTS)]
        xnum_loaded = [sem(f"xnum_loaded{p}") for p in range(2)]
        gathered = [[sem(f"gathered{p}{g}") for g in range(GROUPS)] for p in range(2)]
        gather_open = sem("gather_open")
        stored = sem("stored")
        first_row_ready = sem("first_row_ready")
        ident_zero = sem("ident_zero")
        ident_ready = sem("ident_ready")
        rows_step = sem("rows_step")
        rows_ready = sem("rows_ready")
        wnum_round = sem("wnum_round")
        wnum_ready = sem("wnum_ready")
        vnum_sq_ready = sem("vnum_sq_ready")
        w_hi_ready = sem("w_hi_ready")
        w_lo_ready = sem("w_lo_ready")
        xnum_round = sem("xnum_round")
        xnum_ready = sem("xnum_ready")
        x_turned = sem("x_turned")
        x_hi_ready = sem("x_hi_ready")
        x_lo_ready = sem("x_lo_ready")
        x_used = sem("x_used")
        acc_done = [sem(f"acc_done{h}") for h in range(HALVES)]
        h1_taken = [sem(f"h1_taken{h}") for h in range(HALVES)]
        h_turned = sem("h_turned")
        h_hi_ready = sem("h_hi_ready")
        h_lo_ready = sem("h_lo_ready")
        l2_done = sem("l2_done")
        h2_taken = sem("h2_taken")
        l3_done = sem("l3_done")
        fm_done = sem("fm_done")
        z_free = sem("z_free")
        sum_early = sem("sum_early")
        sum_pairs = sem("sum_pairs")
        sum_done = sem("sum_done")
        sq_done = sem("sq_done")
        squares_ready = sem("squares_ready")
        deep_done = sem("deep_done")
        total_ready = sem("total_ready")
        ssq_ready = sem("ssq_ready")
        inter_ready = sem("inter_ready")
        y_ready = sem("y_ready")

        def slot(p, g):
            return (p * GROUPS + g) % 2

        def group_no(t, g):
            return t * GROUPS + g

        def pairs(p, k0, k1):
            return emb[p][:, :].rearrange("b (k e) -> b k e", e=PAIR)[:, k0:k1, :]

        def chunk_slot(j):
            return j % RAW_SLOTS

        def chunk_raw(j):
            return raw[:, chunk_slot(j) * H1:(chunk_slot(j) + 1) * H1]

        def chunk_split(j):
            if j < KB:
                return w1_hi[:, j, :], w1_lo[:, j, :]
            if j < KB + W2_CHUNKS:
                b = (j - KB) * W2_CHUNK
                return [w[:, b:b + W2_CHUNK, :].rearrange("p b n -> p (b n)") for w in (w2_hi, w2_lo)]
            return [w[:, :, :].rearrange("p b n -> p (b n)") for w in (w3_hi, w3_lo)]

        def chunks_before(n):
            return range(SPLIT_BEFORE[n - 1] if n else 0, SPLIT_BEFORE[n]) if n < len(SPLIT_BEFORE) else []

        block = ctx.enter_context(nc.Block())

        @block.sync
        def _(sp):
            sp.dma_start(cat[:, :], x_cat).then_inc(cat_loaded, 16)

            def load_xnum(t, p):
                sp.dma_start(xnum[p][:, :], x_num[:, bass.ds(t * P, P)]).then_inc(xnum_loaded[p], 16)

            def load_chunk(j):
                if j >= IN_FLIGHT:
                    sp.wait_ge(chunk_loaded[chunk_slot(j - IN_FLIGHT)], 16 * ((j - IN_FLIGHT) // RAW_SLOTS + 1))
                if j >= RAW_SLOTS:
                    sp.wait_ge(w_lo_ready, j - RAW_SLOTS + 1)
                if j < KB:
                    src = W1[j * P:(j + 1) * P, :]
                    dst = chunk_raw(j)
                elif j < KB + W2_CHUNKS:
                    b = (j - KB) * W2_CHUNK
                    src = W2.rearrange("(b p) n -> p b n", p=P)[:, b:b + W2_CHUNK, :]
                    dst = chunk_raw(j).rearrange("p (b n) -> p b n", n=H2)
                else:
                    src = W3.rearrange("(b p) n -> p b n", p=P)
                    dst = chunk_raw(j).rearrange("p (b n) -> p b n", n=H3)
                sp.dma_start(dst, src).then_inc(chunk_loaded[chunk_slot(j)], 16)

            sp.dma_start(wnum_raw, w_num).then_inc(wnum_loaded, 16)
            load_xnum(0, 0)
            for j in range(RAW_SLOTS):
                load_chunk(j)
            load_xnum(1, 1)
            for j in range(RAW_SLOTS, CHUNKS):
                load_chunk(j)
            sp.dma_start(vectors_all[:, :], vectors.to_broadcast((P, H2 + 2 * H3))).then_inc(vectors_loaded, 16)
            with sp.Fori(0, (TILES - 2) // 2) as i:
                for p in range(2):
                    sp.wait_ge(xnum_ready, 2 * i + p + 1)
                    load_xnum(2 * i + p + 2, p)
            sp.wait_ge(y_ready, TILES)
            sp.dma_start(out, y[:, :]).then_inc(stored, 16)
            sp.wait_ge(stored, 16)

        @block.gpsimd
        def _(pool):
            pool.iota(first_row[:, :].rearrange("p (t f) -> p t f", f=FIELDS),
                      pattern=[[0, TILES], [VOCAB, FIELDS]], base=0, channel_multiplier=0).then_inc(first_row_ready, 1)
            pool.memset(ident[:, :], 0.0).then_inc(ident_zero, 1)
            pool.wait_ge(ident_zero, 1)
            pool.affine_select(out=ident[:, :], in_=ident[:, :], compare_op=ALU.not_equal, fill=1.0, base=0,
                               pattern=[[-1, P]], channel_multiplier=1).then_inc(ident_ready, 1)

            def gather(t, p):
                pool.wait_ge(rows_ready, t + 1)
                pool.sem_inc(gather_open, 1)
                for f in range(FIELDS):
                    pool.indirect_dma_start(
                        emb[p][:, f * ROW:(f + 1) * ROW], None, table,
                        bass.IndirectOffsetOnAxis(ap=rows[p][:, f:f + 1], axis=0),
                    ).then_inc(gathered[p][f // 4], GATHERED)

            gather(0, 0)
            pool.wait_ge(wnum_ready, 1)
            pool.wait_ge(vnum_sq_ready, 1)
            gather(1, 1)
            with pool.Fori(0, (TILES - 2) // 2) as i:
                for p in range(2):
                    pool.wait_ge(x_turned, group_no(2 * i + p + 1, 0))
                    pool.wait_ge(sum_done, 2 * i + p + 1)
                    pool.wait_ge(sq_done, 2 * i + p + 1)
                    gather(2 * i + p + 2, p)

        @block.tensor
        def _(pe):
            def turn_x(t, p, g, use):
                pe.wait_ge(gathered[p][g], 2 * len(BLOCKS[g]) * GATHERED * use)
                for n, k in enumerate(BLOCKS[g]):
                    mm = pe.transpose(xT[slot(p, g)][:, n * P:(n + 1) * P], pairs(p, k, k + 1)[:, 0, 1:1 + P],
                                      ident[:, :])
                mm.then_inc(x_turned, 1)

            def layer1_num(t, p):
                pe.wait_ge(xnum_ready, t + 1)
                for h in range(HALVES):
                    pe.matmul(acc[p][h][:, :], xnum_r[p][:, :], wnum[:, h * BANK:(h + 1) * BANK],
                              start=True, stop=False)

            def layer1(t, p, g, split_waits=False, between=None):
                s, last = slot(p, g), g == GROUPS - 1
                pe.wait_ge(x_hi_ready, group_no(t, g) + 1)
                for h in range(HALVES):
                    cols = slice(h * BANK, (h + 1) * BANK)
                    for n, k in enumerate(BLOCKS[g]):
                        if split_waits and h == 0:
                            pe.wait_ge(w_lo_ready, k + 1)
                        xh = x_hi[s][:, n * P:(n + 1) * P]
                        pe.matmul(acc[p][h][:, :], xh, w1_hi[:, k, cols], start=False, stop=False)
                        pe.matmul(acc[p][h][:, :], xh, w1_lo[:, k, cols], start=False, stop=False)
                    if h == 0:
                        pe.wait_ge(x_lo_ready, group_no(t, g) + 1)
                    for n, k in enumerate(BLOCKS[g]):
                        mm = pe.matmul(acc[p][h][:, :], x_lo[s][:, n * P:(n + 1) * P], w1_hi[:, k, cols],
                                       start=False, stop=last and k == BLOCKS[g][-1])
                    if last:
                        mm.then_inc(acc_done[h], 1)
                    if h == 0 and between:
                        between()
                if not last:
                    mm.then_inc(x_used, 1)

            def turn_h1(t, half, bank):
                pe.wait_ge(h1_taken[half], t + 1)
                for n in range(BANK // P):
                    mm = pe.transpose(bank[:, n * P:(n + 1) * P], h1[:, half * BANK + n * P:half * BANK + (n + 1) * P],
                                      ident[:, :])
                mm.then_inc(h_turned, 1)

            def layer2(t, ks, bank, c0=0, c1=H2):
                for k in ks:
                    if k % W2_CHUNK == 0 or k == ks[0]:
                        pe.wait_ge(w_lo_ready, KB + k // W2_CHUNK + 1)
                    half, n = divmod(k, BANK // P)
                    hh, hl = (h[half][:, n * P:(n + 1) * P] for h in (hT_hi, hT_lo))
                    if n == 0:
                        pe.wait_ge(h_hi_ready, 3 * t + half + 1)
                    pe.matmul(bank[:, 0:c1 - c0], hh, w2_hi[:, k, c0:c1], start=(k == 0), stop=False)
                    pe.matmul(bank[:, 0:c1 - c0], hh, w2_lo[:, k, c0:c1], start=False, stop=False)
                    if n == 0:
                        pe.wait_ge(h_lo_ready, 3 * t + half + 1)
                    mm = pe.matmul(bank[:, 0:c1 - c0], hl, w2_hi[:, k, c0:c1], start=False, stop=(k == H1 // P - 1))
                if ks[-1] == H1 // P - 1:
                    mm.then_inc(l2_done, 1)

            def turn_h2(taken, bank, c0=0, c1=H2):
                pe.wait_ge(h2_taken, taken)
                for n in range((c1 - c0) // P):
                    mm = pe.transpose(bank[:, n * P:(n + 1) * P], h2[:, c0 + n * P:c0 + (n + 1) * P], ident[:, :])
                mm.then_inc(h_turned, 1)

            def fm_numeric(t, p, bank):
                pe.matmul(bank[:, Z_FM:Z_FM + FM_COLS], xnum_r[p][:, :], wnum[:, C_FM:C_FM + FM_COLS],
                          start=True, stop=True)
                pe.matmul(bank[:, Z_SQ:Z_SQ + 1], xnum_sq[p][:, :], vnum_sq[:, :], start=True,
                          stop=True).then_inc(fm_done, 1)

            def layer3(split, ks, hi, lo, bank):
                pe.wait_ge(h_hi_ready, split)
                for n, k in enumerate(ks):
                    hh, hl = hi[:, n * P:(n + 1) * P], lo[:, n * P:(n + 1) * P]
                    pe.matmul(bank[:, 0:H3], hh, w3_hi[:, k, :], start=(k == 0), stop=False)
                    pe.matmul(bank[:, 0:H3], hh, w3_lo[:, k, :], start=False, stop=False)
                    if n == 0:
                        pe.wait_ge(h_lo_ready, split)
                    mm = pe.matmul(bank[:, 0:H3], hl, w3_hi[:, k, :], start=False, stop=(k == H2 // P - 1))
                if ks[-1] == H2 // P - 1:
                    mm.then_inc(l3_done, 1)

            def tile(t, p, use, first=False):
                turn_x(t, p, 0, use)
                if first:
                    pe.wait_ge(wnum_ready, 1)
                    pe.wait_ge(vnum_sq_ready, 1)
                layer1_num(t, p)
                if not first:
                    turn_h1(t - 1, 0, hT)
                for g in range(GROUPS):
                    if not first:
                        if g == 1:
                            pe.wait_ge(h_lo_ready, 3 * (t - 1) + 1)
                            turn_h1(t - 1, 1, hT)
                            pe.wait_ge(z_free, t)
                            layer2(t - 1, [0, 1, 2], Z)
                        if g == 2:
                            layer2(t - 1, [3, 4, 5], Z)
                        if g == 3:
                            layer2(t - 1, [6, 7], Z)
                        if g == 4:
                            turn_h2(t, hT)
                        if g == 5:
                            fm_numeric(t - 1, 1 - p, Z)
                            pe.wait_ge(w_lo_ready, CHUNKS)
                            layer3(3 * t, range(H2 // P), hT_hi[0], hT_lo[0], Z)
                    if g < GROUPS - 1:
                        layer1(t, p, g, first, lambda: turn_x(t, p, g + 1, use))
                    else:
                        layer1(t, p, g, first)

            pe.wait_ge(ident_ready, 1)
            tile(0, 0, 1, first=True)
            with pe.Fori(0, (TILES - 2) // 2) as i:
                tile(2 * i + 1, 1, i + 1)
                tile(2 * i + 2, 0, i + 2)
            t, p = TILES - 1, (TILES - 1) % 2
            tile(t, p, TILES // 2)
            fm_numeric(t, p, acc[1 - p][1])
            turn_h1(t, 0, hT)
            turn_h1(t, 1, xT[0])
            layer2(t, range(H1 // P), acc[1 - p][0], 0, H2 // 2)
            layer2(t, range(H1 // P), acc[p][0], H2 // 2, H2)
            pe.wait_ge(z_free, t + 1)
            for half in range(2):
                turn_h2(t + 1 + half, [xT[1], hT][half], half * H2 // 2, (half + 1) * H2 // 2)
            for half in range(2):
                layer3(3 * (t + 1) + half, range(2 * half, 2 * half + 2), x_hi[half], x_lo[half], Z)

        @block.scalar
        def _(act):
            def split_hi(j):
                act.wait_ge(chunk_loaded[chunk_slot(j)], 16 * (j // RAW_SLOTS + 1))
                act.activation(chunk_split(j)[0], chunk_raw(j), ACT.Copy).then_inc(w_hi_ready, 1)

            def x_part(t, p, g, first=False):
                s, n = slot(p, g), len(BLOCKS[g]) * P
                act.wait_ge(x_turned, group_no(t, g) + 1)
                if g >= 2:
                    act.wait_ge(x_used, x_uses(t, g - 2))
                elif not first:
                    if g == 0:
                        act.wait_ge(x_used, x_uses(t - 1, GROUPS - 2))
                    else:
                        act.wait_ge(acc_done[1], t)
                act.activation(x_hi[s][:, 0:n], xT[s][:, 0:n], ACT.Copy).then_inc(x_hi_ready, 1)

            def x_uses(t, g):
                return t * (GROUPS - 1) + g + 1

            def take_h1(t, p):
                act.wait_ge(acc_done[0], t + 1)
                act.activation(h1[:, 0:BANK], acc[p][0][:, :], ACT.Copy).then_inc(h1_taken[0], 1)

            def h_part(turned, bank, hi):
                act.wait_ge(h_turned, turned)
                act.activation(hi, bank, ACT.Relu).then_inc(h_hi_ready, 1)

            def squares(p, n, out=sq_out):
                k0, k1 = [(0, EARLY), (EARLY, KB)][n]
                op = act.activation(out[n].rearrange("b (k e) -> b k e", e=P),
                                    pairs(p, k0, k1)[:, :, 1:1 + P], ACT.Square, accum_out=emb_sq[p][:, n:n + 1])
                if n == 1:
                    op.then_inc(sq_done, 1)

            def tile(t, p, first=False):
                def split_chunks(n):
                    if first:
                        for j in chunks_before(GROUPS + n):
                            split_hi(j)

                take_h1(t - 1, 1 - p)
                split_chunks(0)
                x_part(t, p, 0)
                h_part(3 * t - 2, hT[:, :], hT_hi[0][:, :])
                split_chunks(1)
                x_part(t, p, 1)
                h_part(3 * t - 1, hT[:, :], hT_hi[1][:, :])
                split_chunks(2)
                x_part(t, p, 2)
                split_chunks(3)
                x_part(t, p, 3)
                x_part(t, p, 4)
                h_part(3 * t, hT[:, :], hT_hi[0][:, :])
                x_part(t, p, 5)
                if first:
                    act.wait_ge(w_lo_ready, CHUNKS)
                else:
                    act.wait_ge(squares_ready, t - 1)
                squares(p, 0)
                x_part(t, p, 6)
                squares(p, 1)

            act.wait_ge(wnum_loaded, 16)
            act.activation(wnum[:, :], wnum_raw, ACT.Copy).then_inc(wnum_round, 1)
            for g in range(GROUPS):
                for j in chunks_before(g):
                    split_hi(j)
                if g == GROUPS - 1:
                    squares(0, 0, sq_out_0)
                x_part(0, 0, g, first=True)
            squares(0, 1, sq_out_0)
            tile(1, 1, first=True)
            with act.Fori(0, (TILES - 2) // 2) as i:
                for p in range(2):
                    tile(2 * i + 2 + p, p)
            t, p = TILES - 1, (TILES - 1) % 2
            take_h1(t, p)
            h_part(3 * t + 1, hT[:, :], hT_hi[0][:, :])
            h_part(3 * t + 2, xT[0][:, :], hT_hi[1][:, :])
            for half in range(2):
                h_part(3 * t + 3 + half, [xT[1], hT][half][:, 0:H2 // 2], x_hi[half][:, :])

        @block.vector
        def _(dve):
            def row_numbers(a, b, n):
                dve.tensor_scalar(wrap[:, a:b], cat[:, a:b], 0.0, float(VOCAB), ALU.is_lt, ALU.mult).then_inc(rows_step, 1)
                dve.wait_ge(rows_step, 3 * n + 1)
                dve.tensor_tensor(cat[:, a:b], cat[:, a:b], wrap[:, a:b], ALU.add).then_inc(rows_step, 1)
                dve.wait_ge(rows_step, 3 * n + 2)
                dve.tensor_scalar(cat[:, a:b], cat[:, a:b], 0.0, float(VOCAB - 1), ALU.max, ALU.min).then_inc(rows_step, 1)
                dve.wait_ge(rows_step, 3 * n + 3)

            def split_wnum():
                dve.wait_ge(wnum_loaded, 16)
                dve.scalar_tensor_tensor(out=total[0:PART, 0:K], in0=wnum_raw[0:PART, C_FM:C_FM + K], scalar=1.0,
                                         in1=wnum_raw[0:PART, C_FM:C_FM + K], op0=ALU.mult, op1=ALU.mult,
                                         accum_out=vnum_sq[:, :]).then_inc(vnum_sq_ready, 1)
                dve.wait_ge(wnum_round, 1)
                dve.tensor_tensor(wnum[2 * PART:NUM_K, :], wnum_raw[2 * PART:NUM_K, :],
                                  wnum[2 * PART:NUM_K, :].bitcast(F32), ALU.subtract).then_inc(wnum_ready, 1)

            def split_xnum(t, p, use):
                dve.wait_ge(xnum_loaded[p], 16 * use)
                dve.tensor_copy(xnum_r[p][:, :], xnum[p][:, :]).then_inc(xnum_round, 1)
                dve.tensor_tensor(xnum_sq[p][:, :], xnum[p][0:PART, :], xnum[p][0:PART, :], ALU.mult)
                dve.wait_ge(xnum_round, t + 1)
                dve.tensor_tensor(xnum_r[p][PART:2 * PART, :], xnum[p][PART:2 * PART, :],
                                  xnum_r[p][PART:2 * PART, :].bitcast(F32), ALU.subtract).then_inc(xnum_ready, 1)

            def split_lo(j):
                hi, lo = chunk_split(j)
                dve.wait_ge(w_hi_ready, j + 1)
                dve.tensor_tensor(lo, chunk_raw(j), hi.bitcast(F32), ALU.subtract).then_inc(w_lo_ready, 1)

            def take_rows(t, p):
                dve.tensor_copy(rows[p][:, :], cat[:, bass.ds(t * FIELDS, FIELDS)]).then_inc(rows_ready, 1)

            def x_part(t, p, g):
                s, n = slot(p, g), len(BLOCKS[g]) * P
                dve.wait_ge(x_hi_ready, group_no(t, g) + 1)
                dve.tensor_tensor(x_lo[s][:, 0:n], xT[s][:, 0:n], x_hi[s][:, 0:n].bitcast(F32),
                                  ALU.subtract).then_inc(x_lo_ready, 1)

            def take_h1(t, p):
                dve.wait_ge(acc_done[1], t + 1)
                dve.tensor_copy(h1[:, BANK:H1], acc[p][1][:, :]).then_inc(h1_taken[1], 1)

            def take_h2(l2, bank, c0=0, c1=H2):
                dve.wait_ge(l2_done, l2)
                dve.tensor_tensor(h2[:, c0:c1], bank[:, 0:c1 - c0], b2[:, c0:c1], ALU.add).then_inc(h2_taken, 1)

            def h_part(split, bank, hi, lo):
                dve.wait_ge(h_hi_ready, split)
                dve.scalar_tensor_tensor(out=lo, in0=bank, scalar=0.0, in1=hi.bitcast(F32),
                                         op0=ALU.max, op1=ALU.subtract).then_inc(h_lo_ready, 1)

            def sum_most(p):
                dve.tensor_reduce(pair_sum[:, :], pairs(p, 0, EARLY).rearrange("b k e -> b e k"), AX_X,
                                  ALU.add).then_inc(sum_early, 1)

            def sum_rest(t, p):
                dve.wait_ge(sum_early, t + 1)
                dve.tensor_tensor(pair_sum[:, :], pair_sum[:, :], pairs(p, KB - 1, KB)[:, 0, :],
                                  ALU.add).then_inc(sum_pairs, 1)
                dve.wait_ge(sum_pairs, t + 1)
                dve.tensor_tensor(emb_sum[p][:, 0:K], pair_sum[:, 1:1 + K], pair_sum[:, 1 + K:1 + 2 * K], ALU.add)
                dve.tensor_tensor(emb_sum[p][:, K:ROW], pair_sum[:, 0:1], pair_sum[:, PAIR - 1:PAIR],
                                  ALU.add).then_inc(sum_done, 1)

            def fm_read(t, p, bank):
                dve.wait_ge(fm_done, t + 1)
                dve.wait_ge(sum_done, t + 1)
                dve.tensor_tensor(total[:, :], emb_sum[p][:, :], bank[:, Z_FM:Z_FM + ROW], ALU.add).then_inc(total_ready, 1)
                dve.wait_ge(sq_done, t + 1)
                dve.scalar_tensor_tensor(out=score[:, 2:3], in0=bank[:, Z_SQ:Z_SQ + 1], scalar=emb_sq[p][:, 0:1],
                                         in1=emb_sq[p][:, 1:2], op0=ALU.add, op1=ALU.add).then_inc(squares_ready, 1)

            def deep_read(t):
                dve.wait_ge(l3_done, t + 1)
                dve.tensor_tensor(deep_in, Z[:, 0:H3], b3, ALU.add).then_inc(z_free, 1)

            def fm_score(t):
                dve.wait_ge(total_ready, t + 1)
                dve.scalar_tensor_tensor(out=ssq_out, in0=total[:, 0:K], scalar=1.0, in1=total[:, 0:K], op0=ALU.mult,
                                         op1=ALU.mult, accum_out=score[:, 0:1]).then_inc(ssq_ready, 1)
                dve.wait_ge(squares_ready, t + 1)
                dve.wait_ge(ssq_ready, t + 1)
                dve.tensor_scalar(score[:, 3:4], score[:, 0:1], score[:, 2:3], 0.5, ALU.subtract,
                                  ALU.mult).then_inc(inter_ready, 1)

            def deep_score(t):
                dve.wait_ge(z_free, t + 2)
                dve.scalar_tensor_tensor(out=deep_out, in0=deep_in, scalar=0.0, in1=wo, op0=ALU.max,
                                         op1=ALU.mult, accum_out=score[:, 1:2]).then_inc(deep_done, 1)
                dve.wait_ge(deep_done, t + 1)
                dve.wait_ge(inter_ready, t + 1)
                dve.scalar_tensor_tensor(out=y[:, bass.ds(t, 1)], in0=score[:, 3:4], scalar=total[:, K:ROW],
                                         in1=score[:, 1:2], op0=ALU.add, op1=ALU.add).then_inc(y_ready, 1)

            def tile(t, p, use, first=False):
                staging = not isinstance(use, int) or use > 0

                def split_chunks(n):
                    if first:
                        for j in chunks_before(GROUPS + n):
                            split_lo(j)

                take_h1(t - 1, 1 - p)
                split_chunks(0)
                x_part(t, p, 0)
                h_part(3 * t - 2, hT[:, :], hT_hi[0][:, :], hT_lo[0][:, :])
                split_chunks(1)
                if not first:
                    fm_read(t - 2, p, Z)
                    deep_read(t - 2)
                x_part(t, p, 1)
                h_part(3 * t - 1, hT[:, :], hT_hi[1][:, :], hT_lo[1][:, :])
                if not first:
                    fm_score(t - 2)
                    deep_score(t - 2)
                else:
                    sum_most(1 - p)
                    sum_rest(t - 1, 1 - p)
                split_chunks(2)
                x_part(t, p, 2)
                split_chunks(3)
                x_part(t, p, 3)
                if first:
                    dve.wait_ge(vectors_loaded, 16)
                take_h2(t, Z)
                x_part(t, p, 4)
                h_part(3 * t, hT[:, :], hT_hi[0][:, :], hT_lo[0][:, :])
                x_part(t, p, 5)
                sum_most(p)
                if staging:
                    stage_next(t + 1, 1 - p, use)
                x_part(t, p, 6)
                sum_rest(t, p)

            def stage_next(t, p, use):
                dve.wait_ge(l3_done, t - 1)
                split_xnum(t, p, use)

            dve.wait_ge(cat_loaded, 16)
            dve.wait_ge(first_row_ready, 1)
            row_numbers(0, FIELDS, 0)
            dve.tensor_tensor(rows[0][:, :], cat[:, 0:FIELDS], first_row[:, 0:FIELDS], ALU.add).then_inc(rows_ready, 1)
            row_numbers(FIELDS, TILES * FIELDS, 1)
            dve.tensor_tensor(cat[:, FIELDS:], cat[:, FIELDS:], first_row[:, FIELDS:], ALU.add).then_inc(rows_step, 1)
            dve.wait_ge(rows_step, 7)
            take_rows(1, 1)
            split_wnum()
            split_xnum(0, 0, 1)
            for g in range(GROUPS):
                for j in chunks_before(g):
                    split_lo(j)
                if g == GROUPS - 1:
                    split_xnum(1, 1, 1)
                x_part(0, 0, g)
            dve.memset(score[:, :], 0.0).then_inc(z_free, 1)
            take_rows(2, 0)
            tile(1, 1, 2, first=True)
            with dve.Fori(0, (TILES - 4) // 2) as i:
                for p in range(2):
                    t = 2 * i + 2 + p
                    take_rows(t + 1, 1 - p)
                    tile(t, p, i + 2 + p)
            t = TILES - 2
            take_rows(t + 1, 1)
            tile(t, 0, TILES // 2)
            t, p = TILES - 1, (TILES - 1) % 2
            tile(t, p, 0)
            take_h1(t, p)
            h_part(3 * t + 1, hT[:, :], hT_hi[0][:, :], hT_lo[0][:, :])
            h_part(3 * t + 2, xT[0][:, :], hT_hi[1][:, :], hT_lo[1][:, :])
            fm_read(t - 1, 1 - p, Z)
            deep_read(t - 1)
            fm_score(t - 1)
            deep_score(t - 1)
            dve.wait_ge(y_ready, t)
            fm_read(t, p, acc[1 - p][1])
            fm_score(t)
            take_h2(t + 1, acc[1 - p][0], 0, H2 // 2)
            take_h2(t + 2, acc[p][0], H2 // 2, H2)
            for half in range(2):
                h_part(3 * t + 3 + half, [xT[1], hT][half][:, 0:H2 // 2], x_hi[half][:, :], x_lo[half][:, :])
            deep_read(t)
            deep_score(t)


def kernel(r_x_num, r_x_cat, L0_rec_bias, L0_rec_w_num, L0_rec_lin_cat, L0_rec_v_num, L0_rec_v_cat, L0_rec_W1,
           L0_rec_b1, L0_rec_W2, L0_rec_b2, L0_rec_W3, L0_rec_b3, L0_rec_Wo, L0_rec_bo):
    import numpy as np
    import concourse.bacc as bacc
    from concourse.bass_utils import run_bass_kernel_spmd as run

    table = np.empty((FIELDS, VOCAB, ROW), np.float32)
    table[0::2, :, 0:1], table[0::2, :, 1:] = np.asarray(L0_rec_lin_cat)[0::2], np.asarray(L0_rec_v_cat)[0::2]
    table[1::2, :, :K], table[1::2, :, K:] = np.asarray(L0_rec_v_cat)[1::2], np.asarray(L0_rec_lin_cat)[1::2]
    table = table.reshape(FIELDS * VOCAB, ROW)
    x_part = np.zeros((PART, BATCH), np.float32)
    x_part[:N_NUM] = np.asarray(r_x_num).reshape(P, TILES, N_NUM).transpose(2, 1, 0).reshape(N_NUM, BATCH)
    x_part[N_NUM:N_NUM + 2] = 1.0
    w_part = np.zeros((PART, NUM_COLS), np.float32)
    w_part[:N_NUM, :H1] = np.asarray(L0_rec_W1)[:N_NUM]
    w_part[N_NUM, :H1] = np.asarray(L0_rec_b1)
    w_part[:N_NUM, C_FM:C_FM + K] = np.asarray(L0_rec_v_num)
    w_part[:N_NUM, C_FM + K] = np.asarray(L0_rec_w_num)[:, 0]
    w_part[N_NUM, C_FM + K] = np.asarray(L0_rec_bias)[0]
    w_part[N_NUM + 1, C_FM + K] = np.asarray(L0_rec_bo)[0]
    arrays = {
        "table": table,
        "x_cat": np.asarray(r_x_cat).reshape(P, TILES * FIELDS),
        "x_num": np.concatenate([x_part] * 3),
        "w_num": np.concatenate([w_part] * 3),
        "W1": np.asarray(L0_rec_W1)[N_NUM:],
        "W2": np.asarray(L0_rec_W2),
        "W3": np.asarray(L0_rec_W3),
        "vectors": np.concatenate([np.asarray(a).reshape(-1) for a in (L0_rec_b2, L0_rec_b3, L0_rec_Wo)]).reshape(1, -1),
    }
    nc = bacc.Bacc("TRN2", target_bir_lowering=False, num_devices=1)
    arrays = {f"in_{name}": np.ascontiguousarray(a) for name, a in arrays.items()}
    args = [nc.dram_tensor(name, a.shape, mybir.dt.from_np(a.dtype), kind="ExternalInput").ap()
            for name, a in arrays.items()]
    out = nc.dram_tensor("out", (P, TILES), F32, kind="ExternalOutput").ap()
    deepfm(nc, *args, out)
    return run(nc, [arrays], core_ids=[0]).results[0]["out"].reshape(BATCH, 1)
```

```python
from contextlib import ExitStack

import concourse.bass as bass
from concourse import mybir

F32 = mybir.dt.float32
F32R = mybir.dt.float32r
I32 = mybir.dt.int32
ALU = mybir.AluOpType
ACT = mybir.ActivationFunctionType
AX_X = mybir.AxisListType.X

P = 128
BATCH = 1024
TILES = BATCH // P
FIELDS = 26
VOCAB = 12500
K = 64
ROW = K + 1
PAIR = 2 * ROW
N_NUM = 13
H1, H2, H3 = 1024, 512, 256
BANK = 512
HALVES = H1 // BANK

KB = FIELDS // 2
GROUPS = (KB + 1) // 2
BLOCKS = [list(range(2 * g, min(2 * g + 2, KB))) for g in range(GROUPS)]
EARLY = 10

PART = 32
NUM_K = 3 * PART
C_B3 = H1
C_FM = C_B3 + H3
FM_COLS = ROW + 1
NUM_COLS = C_FM + FM_COLS
Z_FM = H3

RAW_SLOTS = 4
W2_CHUNK = H1 // H2
W2_CHUNKS = (H1 // P) // W2_CHUNK
CHUNKS = KB + W2_CHUNKS + 1
IN_FLIGHT = 2
SPLIT_BEFORE = [3, 5, 8, 10, 12, 14, 15, 16, 17, 18]
LATE_TURNS = (3, 4)
GATHERED = 16


def deepfm(nc, table, x_cat, x_num_rows, x_num, v_num, w_num, W1, W2, W3, vectors, out):
    with ExitStack() as ctx:
        def sb(name, shape, dt=F32):
            return ctx.enter_context(nc.sbuf_tensor(name, shape, dt))

        def sem(name):
            return ctx.enter_context(nc.semaphore(name))

        raw = sb("raw", [P, RAW_SLOTS * H1])
        w1_hi = sb("w1_hi", [P, KB, H1], F32R)
        w1_lo = sb("w1_lo", [P, KB, H1], F32R)
        w2_hi = sb("w2_hi", [P, H1 // P, H2], F32R)
        w2_lo = sb("w2_lo", [P, H1 // P, H2], F32R)
        w3_hi = sb("w3_hi", [P, H2 // P, H3], F32R)
        w3_lo = sb("w3_lo", [P, H2 // P, H3], F32R)
        wnum = sb("wnum", [NUM_K, NUM_COLS], F32R)
        vectors_all = sb("vectors_all", [P, H2 + H3])
        b2, wo = vectors_all[:, 0:H2], vectors_all[:, H2:]
        num_sq = sb("num_sq", [P, TILES])
        ident = sb("ident", [P, P])
        cat = sb("cat", [P, TILES * FIELDS], I32)
        wrap = sb("wrap", [P, TILES * FIELDS], I32)
        first_row = sb("first_row", [P, TILES * FIELDS], I32)
        rows = [sb(f"rows{p}", [P, FIELDS], I32) for p in range(2)]
        emb = [sb(f"emb{p}", [P, FIELDS * ROW]) for p in range(2)]
        xnum = [sb(f"xnum{p}", [NUM_K, P]) for p in range(2)]
        xnum_r = [sb(f"xnum_r{p}", [NUM_K, P], F32R) for p in range(2)]
        x_hi = [sb(f"x_hi{s}", [P, 2 * P], F32R) for s in range(2)]
        x_lo = [sb(f"x_lo{s}", [P, 2 * P], F32R) for s in range(2)]
        h = sb("h", [P, H1 + H2])
        h1, h2 = h[:, 0:H1], h[:, H1:]
        hT_hi = [sb(f"hT_hi{s}", [P, BANK], F32R) for s in range(2)]
        hT_lo = [sb(f"hT_lo{s}", [P, BANK], F32R) for s in range(2)]
        pair_sum = sb("pair_sum", [P, PAIR])
        pair_rest = sb("pair_rest", [P, PAIR])
        emb_sum = sb("emb_sum", [P, ROW])
        emb_sq = sb("emb_sq", [P, 1])
        total = sb("total", [P, ROW])
        score = sb("score", [P, 4])
        y = sb("y", [P, TILES])
        wnum_raw = emb[1][0:NUM_K, 0:NUM_COLS]
        at, scratch = 0, []
        for size in (KB * P, H3, K, N_NUM * K, N_NUM, TILES * N_NUM):
            scratch.append(raw[:, at:at + size])
            at += size
        sq_out, deep_out, ssq_out, vnum_all, vnum_sq, xnum_rows = scratch

        acc = [[ctx.enter_context(nc.psum_tensor(f"acc{p}{h}", [P, BANK], F32)) for h in range(HALVES)]
               for p in range(2)]
        xT = [ctx.enter_context(nc.psum_tensor(f"xT{s}", [P, BANK], F32)) for s in range(2)]
        hT = ctx.enter_context(nc.psum_tensor("hT", [P, BANK], F32))
        Z = ctx.enter_context(nc.psum_tensor("Z", [P, BANK], F32))

        cat_loaded = sem("cat_loaded")
        wnum_loaded = sem("wnum_loaded")
        vectors_loaded = sem("vectors_loaded")
        chunk_loaded = [sem(f"chunk_loaded{s}") for s in range(RAW_SLOTS)]
        xnum_loaded = [sem(f"xnum_loaded{p}") for p in range(2)]
        gathered = [[sem(f"gathered{p}{g}") for g in range(GROUPS)] for p in range(2)]
        gather_open = sem("gather_open")
        stored = sem("stored")
        first_row_ready = sem("first_row_ready")
        ident_zero = sem("ident_zero")
        ident_ready = sem("ident_ready")
        rows_step = sem("rows_step")
        rows_ready = sem("rows_ready")
        wnum_round = sem("wnum_round")
        wnum_ready = sem("wnum_ready")
        num_loaded = sem("num_loaded")
        num_step = sem("num_step")
        w_hi_ready = sem("w_hi_ready")
        w_lo_ready = sem("w_lo_ready")
        xnum_round = sem("xnum_round")
        xnum_ready = sem("xnum_ready")
        x_turned = sem("x_turned")
        x_hi_ready = sem("x_hi_ready")
        x_lo_ready = sem("x_lo_ready")
        x_used = sem("x_used")
        acc_done = [sem(f"acc_done{h}") for h in range(HALVES)]
        h1_taken = [sem(f"h1_taken{h}") for h in range(HALVES)]
        h_turned = sem("h_turned")
        h_hi_ready = sem("h_hi_ready")
        h_lo_ready = sem("h_lo_ready")
        l2_done = sem("l2_done")
        h2_taken = sem("h2_taken")
        l3_done = sem("l3_done")
        fm_done = sem("fm_done")
        z_free = sem("z_free")
        pairs_summed = sem("pairs_summed")
        sum_done = sem("sum_done")
        sq_done = sem("sq_done")
        squares_ready = sem("squares_ready")
        total_ready = sem("total_ready")
        ssq_ready = sem("ssq_ready")
        inter_ready = sem("inter_ready")
        y_ready = sem("y_ready")

        def slot(p, g):
            return (p * GROUPS + g) % 2

        def group_no(t, g):
            return t * GROUPS + g

        def pairs(p, k0, k1):
            return emb[p][:, :].rearrange("b (k e) -> b k e", e=PAIR)[:, k0:k1, :]

        def chunk_slot(j):
            return j % RAW_SLOTS

        def chunk_raw(j):
            return raw[:, chunk_slot(j) * H1:(chunk_slot(j) + 1) * H1]

        def chunk_split(j):
            if j < KB:
                return w1_hi[:, j, :], w1_lo[:, j, :]
            if j < KB + W2_CHUNKS:
                b = (j - KB) * W2_CHUNK
                return [w[:, b:b + W2_CHUNK, :].rearrange("p b n -> p (b n)") for w in (w2_hi, w2_lo)]
            return [w[:, :, :].rearrange("p b n -> p (b n)") for w in (w3_hi, w3_lo)]

        def chunks_before(n):
            return range(SPLIT_BEFORE[n - 1] if n else 0, SPLIT_BEFORE[n]) if n < len(SPLIT_BEFORE) else []

        block = ctx.enter_context(nc.Block())

        @block.sync
        def _(sp):
            sp.dma_start(cat[:, :], x_cat).then_inc(cat_loaded, 16)

            def load_xnum(t, p):
                sp.dma_start(xnum[p][:, :], x_num[:, bass.ds(t * P, P)]).then_inc(xnum_loaded[p], 16)

            def load_chunk(j):
                if j >= IN_FLIGHT:
                    sp.wait_ge(chunk_loaded[chunk_slot(j - IN_FLIGHT)], 16 * ((j - IN_FLIGHT) // RAW_SLOTS + 1))
                if j >= RAW_SLOTS:
                    sp.wait_ge(w_lo_ready, j - RAW_SLOTS + 1)
                if j < KB:
                    src = W1[j * P:(j + 1) * P, :]
                    dst = chunk_raw(j)
                elif j < KB + W2_CHUNKS:
                    b = (j - KB) * W2_CHUNK
                    src = W2.rearrange("(b p) n -> p b n", p=P)[:, b:b + W2_CHUNK, :]
                    dst = chunk_raw(j).rearrange("p (b n) -> p b n", n=H2)
                else:
                    src = W3.rearrange("(b p) n -> p b n", p=P)
                    dst = chunk_raw(j).rearrange("p (b n) -> p b n", n=H3)
                sp.dma_start(dst, src).then_inc(chunk_loaded[chunk_slot(j)], 16)

            sp.dma_start(wnum_raw, w_num).then_inc(wnum_loaded, 16)
            load_xnum(0, 0)
            for j in range(RAW_SLOTS):
                load_chunk(j)
            load_xnum(1, 1)
            for j in range(RAW_SLOTS, CHUNKS):
                load_chunk(j)
            sp.dma_start(vectors_all[:, :], vectors.to_broadcast((P, H2 + H3))).then_inc(vectors_loaded, 16)
            sp.wait_ge(w_lo_ready, CHUNKS)
            sp.dma_start(vnum_all, v_num.to_broadcast((P, N_NUM * K))).then_inc(num_loaded, 16)
            sp.dma_start(xnum_rows, x_num_rows).then_inc(num_loaded, 16)
            with sp.Fori(0, (TILES - 2) // 2) as i:
                for p in range(2):
                    sp.wait_ge(xnum_ready, 2 * i + p + 1)
                    load_xnum(2 * i + p + 2, p)
            sp.wait_ge(y_ready, TILES)
            sp.dma_start(out, y[:, :]).then_inc(stored, 16)
            sp.wait_ge(stored, 16)

        @block.gpsimd
        def _(pool):
            pool.iota(first_row[:, :].rearrange("p (t f) -> p t f", f=FIELDS),
                      pattern=[[0, TILES], [VOCAB, FIELDS]], base=0, channel_multiplier=0).then_inc(first_row_ready, 1)
            pool.memset(ident[:, :], 0.0).then_inc(ident_zero, 1)
            pool.wait_ge(ident_zero, 1)
            pool.affine_select(out=ident[:, :], in_=ident[:, :], compare_op=ALU.not_equal, fill=1.0, base=0,
                               pattern=[[-1, P]], channel_multiplier=1).then_inc(ident_ready, 1)

            def gather(t, p):
                pool.wait_ge(rows_ready, t + 1)
                pool.sem_inc(gather_open, 1)
                for f in range(FIELDS):
                    pool.indirect_dma_start(
                        emb[p][:, f * ROW:(f + 1) * ROW], None, table,
                        bass.IndirectOffsetOnAxis(ap=rows[p][:, f:f + 1], axis=0),
                    ).then_inc(gathered[p][f // 4], GATHERED)

            gather(0, 0)
            pool.wait_ge(wnum_ready, 1)
            gather(1, 1)
            with pool.Fori(0, (TILES - 2) // 2) as i:
                for p in range(2):
                    pool.wait_ge(x_turned, group_no(2 * i + p + 1, 0))
                    pool.wait_ge(sum_done, 2 * i + p + 1)
                    pool.wait_ge(sq_done, 2 * i + p + 1)
                    gather(2 * i + p + 2, p)

        @block.tensor
        def _(pe):
            def turn_x(t, p, g, use):
                pe.wait_ge(gathered[p][g], 2 * len(BLOCKS[g]) * GATHERED * use)
                for n, k in enumerate(BLOCKS[g]):
                    mm = pe.transpose(xT[slot(p, g)][:, n * P:(n + 1) * P], pairs(p, k, k + 1)[:, 0, 1:1 + P],
                                      ident[:, :])
                mm.then_inc(x_turned, 1)

            def layer1_num(t, p, h):
                pe.wait_ge(xnum_ready, t + 1)
                pe.matmul(acc[p][h][:, :], xnum_r[p][:, :], wnum[:, h * BANK:(h + 1) * BANK],
                          start=True, stop=False)

            def hi_products(t, p, g, h, split_waits):
                pe.wait_ge(x_hi_ready, group_no(t, g) + 1)
                for n, k in enumerate(BLOCKS[g]):
                    if split_waits and h == 0:
                        pe.wait_ge(w_lo_ready, k + 1)
                    for w in (w1_hi, w1_lo):
                        pe.matmul(acc[p][h][:, :], x_hi[slot(p, g)][:, n * P:(n + 1) * P],
                                  w[:, k, h * BANK:(h + 1) * BANK], start=False, stop=False)

            def lo_products(t, p, g, h):
                last = g == GROUPS - 1
                pe.wait_ge(x_lo_ready, group_no(t, g) + 1)
                for n, k in enumerate(BLOCKS[g]):
                    mm = pe.matmul(acc[p][h][:, :], x_lo[slot(p, g)][:, n * P:(n + 1) * P],
                                   w1_hi[:, k, h * BANK:(h + 1) * BANK], start=False,
                                   stop=last and k == BLOCKS[g][-1])
                if last:
                    mm.then_inc(acc_done[h], 1)
                elif h == HALVES - 1:
                    mm.then_inc(x_used, 1)

            def layer1(t, p, g, use, first):
                late = first and g in LATE_TURNS
                hi_products(t, p, g, 0, first)
                lo_products(t, p, g, 0)
                if not late:
                    turn_x(t, p, g + 1, use)
                hi_products(t, p, g, 1, first)
                if late:
                    turn_x(t, p, g + 1, use)
                lo_products(t, p, g, 1)

            def layer1_end(t, p, use, first, between=None):
                g = GROUPS - 1
                hi_products(t, p, g - 1, 0, first)
                lo_products(t, p, g - 1, 0)
                turn_x(t, p, g, use)
                hi_products(t, p, g - 1, 1, first)
                hi_products(t, p, g, 0, first)
                lo_products(t, p, g, 0)
                lo_products(t, p, g - 1, 1)
                hi_products(t, p, g, 1, first)
                if between:
                    between()
                lo_products(t, p, g, 1)

            def turn_h1(t, half, bank):
                pe.wait_ge(h1_taken[half], t + 1)
                for n in range(BANK // P):
                    mm = pe.transpose(bank[:, n * P:(n + 1) * P], h1[:, half * BANK + n * P:half * BANK + (n + 1) * P],
                                      ident[:, :])
                mm.then_inc(h_turned, 1)

            def layer2(t, ks, bank, c0=0, c1=H2, between=None):
                for k in ks:
                    half, n = divmod(k, BANK // P)
                    if k % W2_CHUNK == 0 or k == ks[0]:
                        pe.wait_ge(w_lo_ready, KB + k // W2_CHUNK + 1)
                    if n == 0 or k == ks[0]:
                        pe.wait_ge(h_hi_ready, 3 * t + half + 1)
                    hh = hT_hi[half][:, n * P:(n + 1) * P]
                    pe.matmul(bank[:, 0:c1 - c0], hh, w2_hi[:, k, c0:c1], start=(k == 0), stop=False)
                    pe.matmul(bank[:, 0:c1 - c0], hh, w2_lo[:, k, c0:c1], start=False, stop=False)
                if between:
                    between()
                for k in ks:
                    half, n = divmod(k, BANK // P)
                    if n == 0 or k == ks[0]:
                        pe.wait_ge(h_lo_ready, 3 * t + half + 1)
                    mm = pe.matmul(bank[:, 0:c1 - c0], hT_lo[half][:, n * P:(n + 1) * P], w2_hi[:, k, c0:c1],
                                   start=False, stop=(k == H1 // P - 1))
                if ks[-1] == H1 // P - 1:
                    mm.then_inc(l2_done, 1)

            def turn_h2(taken, bank, c0=0, c1=H2):
                pe.wait_ge(h2_taken, taken)
                for n in range((c1 - c0) // P):
                    mm = pe.transpose(bank[:, n * P:(n + 1) * P], h2[:, c0 + n * P:c0 + (n + 1) * P], ident[:, :])
                mm.then_inc(h_turned, 1)

            def fm_numeric(p):
                pe.matmul(Z[:, Z_FM:Z_FM + FM_COLS], xnum_r[p][:, :], wnum[:, C_FM:C_FM + FM_COLS],
                          start=True, stop=True).then_inc(fm_done, 1)

            def layer3_bias(p):
                pe.matmul(Z[:, 0:H3], xnum_r[p][:, :], wnum[:, C_B3:C_B3 + H3], start=True, stop=False)

            def layer3(split, ks, hi, lo, between=None):
                pe.wait_ge(h_hi_ready, split)
                for n, k in enumerate(ks):
                    for w in (w3_hi, w3_lo):
                        pe.matmul(Z[:, 0:H3], hi[:, n * P:(n + 1) * P], w[:, k, :], start=False, stop=False)
                if between:
                    between()
                pe.wait_ge(h_lo_ready, split)
                for n, k in enumerate(ks):
                    mm = pe.matmul(Z[:, 0:H3], lo[:, n * P:(n + 1) * P], w3_hi[:, k, :], start=False,
                                   stop=(k == H2 // P - 1))
                if ks[-1] == H2 // P - 1:
                    mm.then_inc(l3_done, 1)

            def tile(t, p, use, first=False, last=False):
                if first:
                    turn_x(t, p, 0, use)
                    pe.wait_ge(wnum_ready, 1)
                layer1_num(t, p, 0)
                if not first:
                    turn_h1(t - 1, 0, hT)
                layer1_num(t, p, 1)
                if not first:
                    turn_h1(t - 1, 1, xT[slot(p, 1)])
                    pe.wait_ge(z_free, t)
                    turn_x(t, p, 0, use)
                    layer2(t - 1, [0, 1, 2], Z)
                for g in range(GROUPS - 2):
                    if not first:
                        if g == 0:
                            layer2(t - 1, [3, 4, 5], Z)
                        if g == 1:
                            layer2(t - 1, [6, 7], Z)
                        if g == 2:
                            turn_h2(t, hT)
                        if g == 3:
                            fm_numeric(1 - p)
                            layer3_bias(1 - p)
                            pe.wait_ge(w_lo_ready, CHUNKS)
                            layer3(3 * t, range(H2 // P), hT_hi[0], hT_lo[0])
                    layer1(t, p, g, use, first)
                layer1_end(t, p, use, first, between=(lambda: turn_h1(t, 0, hT)) if last else None)

            pe.wait_ge(ident_ready, 1)
            tile(0, 0, 1, first=True)
            with pe.Fori(0, (TILES - 2) // 2) as i:
                tile(2 * i + 1, 1, i + 1)
                tile(2 * i + 2, 0, i + 2)
            t, p = TILES - 1, (TILES - 1) % 2
            tile(t, p, TILES // 2, last=True)
            ka, kb = range(0, H1 // P // 2), range(H1 // P // 2, H1 // P)
            bank_a, bank_b = acc[1 - p][0], acc[p][0]
            layer2(t, ka, bank_a, 0, H2 // 2, between=lambda: turn_h1(t, 1, xT[0]))
            pe.wait_ge(z_free, t + 1)
            fm_numeric(p)
            layer2(t, ka, bank_b, H2 // 2, H2)
            layer2(t, kb, bank_a, 0, H2 // 2)
            layer2(t, kb, bank_b, H2 // 2, H2, between=lambda: turn_h2(t + 1, xT[1], 0, H2 // 2))
            pe.wait_ge(total_ready, t + 1)
            layer3_bias(p)
            layer3(3 * (t + 1), [0, 1], x_hi[0], x_lo[0], between=lambda: turn_h2(t + 2, hT, H2 // 2, H2))
            layer3(3 * (t + 1) + 1, [2, 3], x_hi[1], x_lo[1])

        @block.scalar
        def _(act):
            def split_hi(j):
                act.wait_ge(chunk_loaded[chunk_slot(j)], 16 * (j // RAW_SLOTS + 1))
                act.activation(chunk_split(j)[0], chunk_raw(j), ACT.Copy).then_inc(w_hi_ready, 1)

            def x_part(t, p, g, first=False):
                s, n = slot(p, g), len(BLOCKS[g]) * P
                act.wait_ge(x_turned, group_no(t, g) + 1)
                if g >= 2:
                    act.wait_ge(x_used, x_uses(t, g - 2))
                elif not first:
                    if g == 0:
                        act.wait_ge(x_used, x_uses(t - 1, GROUPS - 2))
                    else:
                        act.wait_ge(acc_done[1], t)
                act.activation(x_hi[s][:, 0:n], xT[s][:, 0:n], ACT.Copy).then_inc(x_hi_ready, 1)

            def x_uses(t, g):
                return t * (GROUPS - 1) + g + 1

            def take_h1(t, p):
                act.wait_ge(acc_done[0], t + 1)
                act.activation(h1[:, 0:BANK], acc[p][0][:, :], ACT.Copy).then_inc(h1_taken[0], 1)

            def h_part(turned, bank, hi):
                act.wait_ge(h_turned, turned)
                act.activation(hi, bank, ACT.Relu).then_inc(h_hi_ready, 1)

            def squares(p):
                act.activation(sq_out.rearrange("b (k e) -> b k e", e=P), pairs(p, 0, KB)[:, :, 1:1 + P],
                               ACT.Square, accum_out=emb_sq[:, :]).then_inc(sq_done, 1)

            def tile(t, p, first=False):
                def split_chunks(n):
                    if first:
                        for j in chunks_before(GROUPS + n):
                            split_hi(j)

                take_h1(t - 1, 1 - p)
                h_part(3 * t - 2, hT[:, :], hT_hi[0][:, :])
                h_part(3 * t - 1, xT[slot(p, 1)][:, :], hT_hi[1][:, :])
                split_chunks(0)
                x_part(t, p, 0)
                split_chunks(1)
                x_part(t, p, 1)
                split_chunks(2)
                x_part(t, p, 2)
                h_part(3 * t, hT[:, :], hT_hi[0][:, :])
                split_chunks(3)
                x_part(t, p, 3)
                if first:
                    act.wait_ge(w_lo_ready, CHUNKS)
                else:
                    act.wait_ge(squares_ready, t - 1)
                squares(1 - p)
                x_part(t, p, 4)
                x_part(t, p, 5)
                x_part(t, p, 6)

            act.wait_ge(wnum_loaded, 16)
            act.activation(wnum[:, :], wnum_raw, ACT.Copy).then_inc(wnum_round, 1)
            for g in range(GROUPS):
                for j in chunks_before(g):
                    split_hi(j)
                x_part(0, 0, g, first=True)
            tile(1, 1, first=True)
            with act.Fori(0, (TILES - 2) // 2) as i:
                for p in range(2):
                    tile(2 * i + 2 + p, p)
            t, p = TILES - 1, (TILES - 1) % 2
            take_h1(t, p)
            h_part(3 * t + 1, hT[:, :], hT_hi[0][:, :])
            h_part(3 * t + 2, xT[0][:, :], hT_hi[1][:, :])
            act.wait_ge(squares_ready, t)
            squares(p)
            for half in range(2):
                h_part(3 * t + 3 + half, [xT[1], hT][half][:, 0:H2 // 2], x_hi[half][:, :])

        @block.vector
        def _(dve):
            def row_numbers(a, b, out, done, n):
                dve.tensor_scalar(wrap[:, a:b], cat[:, a:b], 0.0, float(VOCAB), ALU.is_lt,
                                  ALU.mult).then_inc(rows_step, 1)
                dve.wait_ge(rows_step, 2 * n + 1)
                dve.scalar_tensor_tensor(out=cat[:, a:b], in0=cat[:, a:b], scalar=float(VOCAB - 1), in1=wrap[:, a:b],
                                         op0=ALU.min, op1=ALU.add).then_inc(rows_step, 1)
                dve.wait_ge(rows_step, 2 * n + 2)
                dve.scalar_tensor_tensor(out=out, in0=cat[:, a:b], scalar=0.0, in1=first_row[:, a:b],
                                         op0=ALU.max, op1=ALU.add).then_inc(done, 1)

            def split_wnum():
                dve.wait_ge(wnum_loaded, 16)
                dve.wait_ge(wnum_round, 1)
                dve.tensor_tensor(wnum[2 * PART:NUM_K, :], wnum_raw[2 * PART:NUM_K, :],
                                  wnum[2 * PART:NUM_K, :].bitcast(F32), ALU.subtract).then_inc(wnum_ready, 1)

            def split_xnum(t, p, use):
                dve.wait_ge(xnum_loaded[p], 16 * use)
                dve.tensor_copy(xnum_r[p][:, :], xnum[p][:, :]).then_inc(xnum_round, 1)
                dve.wait_ge(xnum_round, t + 1)
                dve.tensor_tensor(xnum_r[p][PART:2 * PART, :], xnum[p][PART:2 * PART, :],
                                  xnum_r[p][PART:2 * PART, :].bitcast(F32), ALU.subtract).then_inc(xnum_ready, 1)

            def square_numbers():
                x = xnum_rows.rearrange("p (t f) -> p t f", f=N_NUM)
                dve.wait_ge(num_loaded, 32)
                dve.tensor_tensor(vnum_all, vnum_all, vnum_all, ALU.mult).then_inc(num_step, 1)
                dve.tensor_tensor(xnum_rows, xnum_rows, xnum_rows, ALU.mult).then_inc(num_step, 1)
                dve.wait_ge(num_step, 2)
                dve.tensor_reduce(vnum_sq, vnum_all.rearrange("p (f k) -> p f k", k=K), AX_X,
                                  ALU.add).then_inc(num_step, 1)
                dve.wait_ge(num_step, 3)
                dve.tensor_tensor(x, x, vnum_sq.unsqueeze(1).to_broadcast((P, TILES, N_NUM)),
                                  ALU.mult).then_inc(num_step, 1)
                dve.wait_ge(num_step, 4)
                dve.tensor_reduce(num_sq[:, :], x, AX_X, ALU.add).then_inc(num_step, 1)

            def split_lo(j):
                hi, lo = chunk_split(j)
                dve.wait_ge(w_hi_ready, j + 1)
                dve.tensor_tensor(lo, chunk_raw(j), hi.bitcast(F32), ALU.subtract).then_inc(w_lo_ready, 1)

            def take_rows(t, p):
                dve.tensor_copy(rows[p][:, :], cat[:, bass.ds(t * FIELDS, FIELDS)]).then_inc(rows_ready, 1)

            def x_part(t, p, g):
                s, n = slot(p, g), len(BLOCKS[g]) * P
                dve.wait_ge(x_hi_ready, group_no(t, g) + 1)
                dve.tensor_tensor(x_lo[s][:, 0:n], xT[s][:, 0:n], x_hi[s][:, 0:n].bitcast(F32),
                                  ALU.subtract).then_inc(x_lo_ready, 1)

            def take_h1(t, p):
                dve.wait_ge(acc_done[1], t + 1)
                dve.tensor_copy(h1[:, BANK:H1], acc[p][1][:, :]).then_inc(h1_taken[1], 1)

            def take_h2(l2, bank, c0=0, c1=H2):
                dve.wait_ge(l2_done, l2)
                dve.tensor_tensor(h2[:, c0:c1], bank[:, 0:c1 - c0], b2[:, c0:c1], ALU.add).then_inc(h2_taken, 1)

            def h_part(split, bank, hi, lo):
                dve.wait_ge(h_hi_ready, split)
                dve.scalar_tensor_tensor(out=lo, in0=bank, scalar=0.0, in1=hi.bitcast(F32),
                                         op0=ALU.max, op1=ALU.subtract).then_inc(h_lo_ready, 1)

            def sum_pairs(p, k0, k1, out):
                dve.tensor_reduce(out[:, :], pairs(p, k0, k1).rearrange("b k e -> b e k"), AX_X,
                                  ALU.add).then_inc(pairs_summed, 1)

            def sum_halves(n):
                dve.wait_ge(pairs_summed, n)
                dve.tensor_tensor(emb_sum[:, 0:K], pair_sum[:, 1:1 + K], pair_sum[:, 1 + K:1 + 2 * K], ALU.add)
                dve.tensor_tensor(emb_sum[:, K:ROW], pair_sum[:, 0:1], pair_sum[:, PAIR - 1:PAIR],
                                  ALU.add).then_inc(sum_done, 1)

            def fm_read(t):
                dve.wait_ge(fm_done, t + 1)
                dve.wait_ge(sum_done, t + 1)
                dve.tensor_tensor(total[:, :], emb_sum[:, :], Z[:, Z_FM:Z_FM + ROW], ALU.add).then_inc(total_ready, 1)
                dve.wait_ge(num_step, 5)
                dve.wait_ge(sq_done, t + 1)
                dve.tensor_tensor(score[:, 2:3], num_sq[:, bass.ds(t, 1)], emb_sq[:, :],
                                  ALU.add).then_inc(squares_ready, 1)

            def deep_read(t):
                dve.wait_ge(l3_done, t + 1)
                dve.scalar_tensor_tensor(out=deep_out, in0=Z[:, 0:H3], scalar=0.0, in1=wo, op0=ALU.max,
                                         op1=ALU.mult, accum_out=score[:, 1:2]).then_inc(z_free, 1)

            def fm_score(t):
                dve.wait_ge(total_ready, t + 1)
                dve.scalar_tensor_tensor(out=ssq_out, in0=total[:, 0:K], scalar=1.0, in1=total[:, 0:K], op0=ALU.mult,
                                         op1=ALU.mult, accum_out=score[:, 0:1]).then_inc(ssq_ready, 1)
                dve.wait_ge(squares_ready, t + 1)
                dve.wait_ge(ssq_ready, t + 1)
                dve.tensor_scalar(score[:, 3:4], score[:, 0:1], score[:, 2:3], 0.5, ALU.subtract,
                                  ALU.mult).then_inc(inter_ready, 1)

            def add_up(t):
                dve.wait_ge(z_free, t + 2)
                dve.wait_ge(inter_ready, t + 1)
                dve.scalar_tensor_tensor(out=y[:, bass.ds(t, 1)], in0=score[:, 3:4], scalar=total[:, K:ROW],
                                         in1=score[:, 1:2], op0=ALU.add, op1=ALU.add).then_inc(y_ready, 1)

            def tile(t, p, use=None, first=False, last=False):
                def split_chunks(n):
                    if first:
                        for j in chunks_before(GROUPS + n):
                            split_lo(j)

                take_h1(t - 1, 1 - p)
                h_part(3 * t - 2, hT[:, :], hT_hi[0][:, :], hT_lo[0][:, :])
                h_part(3 * t - 1, xT[slot(p, 1)][:, :], hT_hi[1][:, :], hT_lo[1][:, :])
                split_chunks(0)
                x_part(t, p, 0)
                split_chunks(1)
                x_part(t, p, 1)
                split_chunks(2)
                if first:
                    dve.wait_ge(vectors_loaded, 16)
                take_h2(t, Z)
                x_part(t, p, 2)
                h_part(3 * t, hT[:, :], hT_hi[0][:, :], hT_lo[0][:, :])
                split_chunks(3)
                x_part(t, p, 3)
                sum_pairs(1 - p, 0, KB, pair_sum)
                sum_halves(t)
                x_part(t, p, 4)
                if first:
                    square_numbers()
                if last:
                    dve.wait_ge(sum_done, t)
                    sum_pairs(p, 0, EARLY, pair_sum)
                x_part(t, p, 5)
                dve.wait_ge(l3_done, t)
                fm_read(t - 1)
                deep_read(t - 1)
                fm_score(t - 1)
                add_up(t - 1)
                if not last:
                    split_xnum(t + 1, 1 - p, use)
                x_part(t, p, 6)

            dve.wait_ge(cat_loaded, 16)
            dve.wait_ge(first_row_ready, 1)
            row_numbers(0, FIELDS, rows[0][:, :], rows_ready, 0)
            row_numbers(FIELDS, TILES * FIELDS, cat[:, FIELDS:], rows_step, 1)
            dve.wait_ge(rows_step, 5)
            take_rows(1, 1)
            split_wnum()
            split_xnum(0, 0, 1)
            for g in range(GROUPS):
                for j in chunks_before(g):
                    split_lo(j)
                if g == GROUPS - 1:
                    split_xnum(1, 1, 1)
                x_part(0, 0, g)
            dve.memset(score[:, :], 0.0).then_inc(z_free, 1)
            take_rows(2, 0)
            tile(1, 1, 2, first=True)
            with dve.Fori(0, (TILES - 4) // 2) as i:
                for p in range(2):
                    t = 2 * i + 2 + p
                    take_rows(t + 1, 1 - p)
                    tile(t, p, i + 2 + p)
            t = TILES - 2
            take_rows(t + 1, 1)
            tile(t, 0, TILES // 2)
            t, p = TILES - 1, (TILES - 1) % 2
            tile(t, p, last=True)
            take_h1(t, p)
            h_part(3 * t + 1, hT[:, :], hT_hi[0][:, :], hT_lo[0][:, :])
            h_part(3 * t + 2, xT[0][:, :], hT_hi[1][:, :], hT_lo[1][:, :])
            sum_pairs(p, EARLY, KB, pair_rest)
            dve.wait_ge(pairs_summed, t + 2)
            dve.tensor_tensor(pair_sum[:, :], pair_sum[:, :], pair_rest[:, :], ALU.add).then_inc(pairs_summed, 1)
            sum_halves(t + 3)
            fm_read(t)
            for half in range(2):
                take_h2(t + 1 + half, [acc[1 - p][0], acc[p][0]][half], half * H2 // 2, (half + 1) * H2 // 2)
                if half == 0:
                    fm_score(t)
                h_part(3 * t + 3 + half, [xT[1], hT][half][:, 0:H2 // 2], x_hi[half][:, :], x_lo[half][:, :])
            deep_read(t)
            add_up(t)


def kernel(r_x_num, r_x_cat, L0_rec_bias, L0_rec_w_num, L0_rec_lin_cat, L0_rec_v_num, L0_rec_v_cat, L0_rec_W1,
           L0_rec_b1, L0_rec_W2, L0_rec_b2, L0_rec_W3, L0_rec_b3, L0_rec_Wo, L0_rec_bo):
    import numpy as np
    import concourse.bacc as bacc
    from concourse.bass_utils import run_bass_kernel_spmd as run

    table = np.empty((FIELDS, VOCAB, ROW), np.float32)
    table[0::2, :, 0:1], table[0::2, :, 1:] = np.asarray(L0_rec_lin_cat)[0::2], np.asarray(L0_rec_v_cat)[0::2]
    table[1::2, :, :K], table[1::2, :, K:] = np.asarray(L0_rec_v_cat)[1::2], np.asarray(L0_rec_lin_cat)[1::2]
    table = table.reshape(FIELDS * VOCAB, ROW)
    x_part = np.zeros((PART, BATCH), np.float32)
    x_part[:N_NUM] = np.asarray(r_x_num).reshape(P, TILES, N_NUM).transpose(2, 1, 0).reshape(N_NUM, BATCH)
    x_part[N_NUM:N_NUM + 2] = 1.0
    w_part = np.zeros((PART, NUM_COLS), np.float32)
    w_part[:N_NUM, :H1] = np.asarray(L0_rec_W1)[:N_NUM]
    w_part[N_NUM, :H1] = np.asarray(L0_rec_b1)
    w_part[N_NUM, C_B3:C_B3 + H3] = np.asarray(L0_rec_b3)
    w_part[:N_NUM, C_FM:C_FM + K] = np.asarray(L0_rec_v_num)
    w_part[:N_NUM, C_FM + K] = np.asarray(L0_rec_w_num)[:, 0]
    w_part[N_NUM, C_FM + K] = np.asarray(L0_rec_bias)[0]
    w_part[N_NUM + 1, C_FM + K] = np.asarray(L0_rec_bo)[0]
    arrays = {
        "table": table,
        "x_cat": np.asarray(r_x_cat).reshape(P, TILES * FIELDS),
        "x_num_rows": np.asarray(r_x_num).reshape(P, TILES * N_NUM),
        "x_num": np.concatenate([x_part] * 3),
        "v_num": np.asarray(L0_rec_v_num).reshape(1, N_NUM * K),
        "w_num": np.concatenate([w_part] * 3),
        "W1": np.asarray(L0_rec_W1)[N_NUM:],
        "W2": np.asarray(L0_rec_W2),
        "W3": np.asarray(L0_rec_W3),
        "vectors": np.concatenate([np.asarray(a).reshape(-1) for a in (L0_rec_b2, L0_rec_Wo)]).reshape(1, -1),
    }
    nc = bacc.Bacc("TRN2", target_bir_lowering=False, num_devices=1)
    arrays = {f"in_{name}": np.ascontiguousarray(a) for name, a in arrays.items()}
    args = [nc.dram_tensor(name, a.shape, mybir.dt.from_np(a.dtype), kind="ExternalInput").ap()
            for name, a in arrays.items()]
    out = nc.dram_tensor("out", (P, TILES), F32, kind="ExternalOutput").ap()
    deepfm(nc, *args, out)
    return run(nc, [arrays], core_ids=[0]).results[0]["out"].reshape(BATCH, 1)
```
